# Optimizing a Trainium2 kernel written in Bass

```python
import numpy as np
import jax
import jax.numpy as jnp

def _softmax(x, axis=-1):
    return jax.nn.softmax(x, axis=axis)

def _gelu(x):
    return jax.nn.gelu(x, approximate=True)

def _silu(x):
    return jax.nn.silu(x)

def _sigmoid(x):
    return jax.nn.sigmoid(x)

def _layernorm(x, axis=-1, eps=1e-05):
    m = jnp.mean(x, axis=axis, keepdims=True)
    v = jnp.var(x, axis=axis, keepdims=True)
    return (x - m) / jnp.sqrt(v + eps)

def _scatter_add(tgt, idx, src, axis=0):
    return tgt.at[idx].add(src)

def _segment_sum(src, seg, n):
    return jax.ops.segment_sum(src, seg, n)
kernel_name = 'mk_adaln_d1_jaxref_r4_3e8f2e'

def setup_inputs(seed: int=0):
    np.random.seed(seed)
    _w = jnp.asarray

    def _L0_attn_setup():
        import jax, jax.numpy as jnp
        import numpy as np
        from jax import lax

        def _causal_depthwise_conv(x, conv_w, conv_b):
            K = conv_w.shape[-1]
            xc = jnp.transpose(x, (0, 2, 1))
            xc = jnp.pad(xc, ((0, 0), (0, 0), (K - 1, 0)))
            D = xc.shape[1]
            y = lax.conv_general_dilated(xc, conv_w, window_strides=(1,), padding='VALID', dimension_numbers=('NCH', 'OIH', 'NCH'), feature_group_count=D)
            y = y + conv_b[None, :, None]
            return jnp.transpose(y, (0, 2, 1))
        key = jax.random.key(seed)
        ks = jax.random.split(key, 7)
        B, L, Dm, S, K = (4, 1024, 512, 128, 4)
        s = 0.02
        x = jax.random.normal(ks[0], (B, L, Dm), dtype=jnp.float32)
        Wxproj = jax.random.normal(ks[1], (2 * S + 1, Dm), dtype=jnp.float32) * s
        Winproj = jax.random.normal(ks[2], (S, Dm), dtype=jnp.float32) * s
        Woutproj = jax.random.normal(ks[3], (Dm, S), dtype=jnp.float32) * s
        conv_w = jax.random.normal(ks[4], (Dm, 1, K), dtype=jnp.float32) * 0.5
        conv_b = jax.random.normal(ks[5], (Dm,), dtype=jnp.float32) * 0.02
        A_log = jnp.log(jnp.arange(1, S + 1, dtype=jnp.float32))
        D = jnp.ones((Dm,), dtype=jnp.float32)
        return {'x': x, 'Wxproj': Wxproj, 'Winproj': Winproj, 'Woutproj': Woutproj, 'conv_w': conv_w, 'conv_b': conv_b, 'A_log': A_log, 'D': D}
    _L0_attn_in = _L0_attn_setup()

    def _L0_ffn_setup():
        import jax, jax.numpy as jnp
        import numpy as np
        DIM = 512
        HIDDEN = 2048
        NUM_EXPERTS = 2
        BATCH, SEQ = (4, 256)
        key = jax.random.key(seed)
        k1, k2, k3, k4 = jax.random.split(key, 4)
        x = jax.random.normal(k1, (BATCH, SEQ, DIM), dtype=jnp.float32)
        w_router = jax.random.normal(k2, (NUM_EXPERTS, DIM), dtype=jnp.float32) * (1.0 / np.sqrt(DIM))
        w_fc = jax.random.normal(k3, (NUM_EXPERTS, HIDDEN, DIM), dtype=jnp.float32) * (1.0 / np.sqrt(DIM))
        w_proj = jax.random.normal(k4, (NUM_EXPERTS, DIM, HIDDEN), dtype=jnp.float32) * (1.0 / np.sqrt(HIDDEN))
        return {'x': x, 'w_router': w_router, 'w_fc': w_fc, 'w_proj': w_proj}
    _L0_ffn_in = _L0_ffn_setup()
    _L0_c = _w((lambda *s: np.random.randn(*s).astype(np.float32) * 0.05)(4, 512))
    _L0_wmod = _w((lambda *s: np.random.randn(*s).astype(np.float32) * 0.05)(512, 6 * 512) * 512 ** (-0.5))
    _d = {'L0_attn_x': _L0_attn_in['x'], 'L0_attn_Wxproj': _L0_attn_in['Wxproj'], 'L0_attn_Winproj': _L0_attn_in['Winproj'], 'L0_attn_Woutproj': _L0_attn_in['Woutproj'], 'L0_attn_conv_w': _L0_attn_in['conv_w'], 'L0_attn_conv_b': _L0_attn_in['conv_b'], 'L0_attn_A_log': _L0_attn_in['A_log'], 'L0_attn_D': _L0_attn_in['D'], 'L0_ffn_w_router': _L0_ffn_in['w_router'], 'L0_ffn_w_fc': _L0_ffn_in['w_fc'], 'L0_ffn_w_proj': _L0_ffn_in['w_proj'], 'L0_c': _L0_c, 'L0_wmod': _L0_wmod}
    _x0 = _d['L0_attn_x']
    _d['L0_attn_x'] = jax.random.normal(jax.random.fold_in(jax.random.key(seed), 1), (4, 512, 512), dtype=_x0.dtype)
    del _x0
    return _d

def reference(L0_attn_x, L0_attn_Wxproj, L0_attn_Winproj, L0_attn_Woutproj, L0_attn_conv_w, L0_attn_conv_b, L0_attn_A_log, L0_attn_D, L0_ffn_w_router, L0_ffn_w_fc, L0_ffn_w_proj, L0_c, L0_wmod):

    def _L0_attn_ref(x, Wxproj, Winproj, Woutproj, conv_w, conv_b, A_log, D):
        import jax, jax.numpy as jnp
        import numpy as np
        from jax import lax

        def _causal_depthwise_conv(x, conv_w, conv_b):
            K = conv_w.shape[-1]
            xc = jnp.transpose(x, (0, 2, 1))
            xc = jnp.pad(xc, ((0, 0), (0, 0), (K - 1, 0)))
            D = xc.shape[1]
            y = lax.conv_general_dilated(xc, conv_w, window_strides=(1,), padding='VALID', dimension_numbers=('NCH', 'OIH', 'NCH'), feature_group_count=D)
            y = y + conv_b[None, :, None]
            return jnp.transpose(y, (0, 2, 1))
        S = A_log.shape[0]
        x_conv = _causal_depthwise_conv(x, conv_w, conv_b)
        ssm_params = jnp.einsum('bld,pd->blp', x, Wxproj)
        Bmat = ssm_params[..., :S]
        Cmat = ssm_params[..., S:2 * S]
        delta = jax.nn.softplus(ssm_params[..., 2 * S:])
        A = -jnp.exp(A_log)
        deltaA = jnp.exp(A[None, None, :] * delta)
        x_state = jnp.einsum('bld,sd->bls', x_conv, Winproj)
        Bu = delta * Bmat * x_state

        def combine(c1, c2):
            a1, b1 = c1
            a2, b2 = c2
            return (a1 * a2, a2 * b1 + b2)
        _, h = lax.associative_scan(combine, (deltaA, Bu), axis=1)
        h_mod = Cmat * h
        out = jnp.einsum('bls,ds->bld', h_mod, Woutproj) + D[None, None, :] * x_conv
        return out

    def _L0_ffn_ref(x, w_router, w_fc, w_proj):
        import jax, jax.numpy as jnp
        import numpy as np
        DIM = 512
        HIDDEN = 2048
        NUM_EXPERTS = 2
        BATCH, SEQ = (4, 256)
        bsz, seq, dim = x.shape
        num_experts = w_router.shape[0]
        x_flat = x.reshape(-1, dim)
        logits = x_flat @ w_router.T
        probs = jax.nn.softmax(logits, axis=-1)
        top_idx = jnp.argmax(probs, axis=-1)
        top_weight = jnp.take_along_axis(probs, top_idx[:, None], axis=1)[:, 0]
        h = jnp.einsum('nd,ehd->enh', x_flat, w_fc)
        a = jnp.square(jnp.where(h >= 0, h, 0.5 * h))
        expert_out = jnp.einsum('enh,edh->end', a, w_proj)
        mask = (top_idx[None, :] == jnp.arange(num_experts)[:, None]).astype(x.dtype)
        out = jnp.einsum('end,en->nd', expert_out, mask * top_weight[None, :])
        return out.reshape(bsz, seq, dim)
    x = L0_attn_x
    mod = (_silu(L0_c) @ L0_wmod).reshape(L0_c.shape[0], 6, 1, -1)
    sa, ca, ga, sb, cb, gb = (mod[:, 0], mod[:, 1], mod[:, 2], mod[:, 3], mod[:, 4], mod[:, 5])
    ga = (2 * (ga >= 0) - 1) * jnp.maximum(jnp.abs(ga), 0.25)
    gb = (2 * (gb >= 0) - 1) * jnp.maximum(jnp.abs(gb), 0.25)
    h = _layernorm(x, axis=-1) * (1 + ca) + sa
    x = x + ga * _L0_attn_ref(h, L0_attn_Wxproj, L0_attn_Winproj, L0_attn_Woutproj, L0_attn_conv_w, L0_attn_conv_b, L0_attn_A_log, L0_attn_D)
    h = _layernorm(x, axis=-1) * (1 + cb) + sb
    x = x + gb * _L0_ffn_ref(h, L0_ffn_w_router, L0_ffn_w_fc, L0_ffn_w_proj)
    return x

_drawn_inputs = setup_inputs


def setup_inputs(seed=0):
    import zlib

    import numpy as np

    out = dict(_drawn_inputs(seed))
    spreads = {'L0_attn_D': (1.0, 0.6)}
    factors = {'L0_attn_Wxproj': 8.0,
     'L0_attn_Winproj': 8.0,
     'L0_attn_Woutproj': 7.459,
     'L0_attn_conv_b': 8.0,
     'L0_attn_A_log': 8.0,
     'L0_ffn_w_router': 8.0,
     'L0_ffn_w_fc': 8.0,
     'L0_ffn_w_proj': 8.0}
    for name, (base, spread) in spreads.items():
        noise = np.random.default_rng([zlib.crc32(name.encode()), seed]).standard_normal(out[name].shape)
        drawn = base * np.exp(spread * noise) if base else spread * noise
        out[name] = jnp.asarray(drawn.astype(out[name].dtype))
    for name, factor in factors.items():
        out[name] = (out[name] * factor).astype(out[name].dtype)
    return out
```

```python
import concourse.bass as bass
from concourse import mybir
import numpy as np
from contextlib import ExitStack

F32 = mybir.dt.float32
F32R = mybir.dt.float32r
I32 = mybir.dt.int32
U32 = mybir.dt.uint32
ALU = mybir.AluOpType
ACT = mybir.ActivationFunctionType

P = 128
NB = 4
L = 512
DM = 512
S = 128
TAPS = 4
PAD = TAPS - 1
HID = 2048
NE = 2
TOK = NB * L
KT = DM // P
TJ = L // P
TILE = 256
SUB = TILE // P
NT = TOK // TILE + 1
ROWS = NT * TILE
HB = 256
NHB = HID // HB
HM = HB // P
CH = 8
ROW = 2 * DM + 8
EPS = 1e-5
NO_TOKEN = 2 * TOK - 1


class Steps:

    def __init__(self, eng, sem, base):
        self.eng, self.sem, self.base, self.n = eng, sem, base, 0

    def mark(self, ins):
        ins.then_inc(self.sem, 1)
        self.n += 1

    def settle(self):
        self.eng.wait_ge(self.sem, self.base + self.n)

    def link(self, ins):
        self.mark(ins)
        self.settle()


def wait(eng, sem, count):
    if isinstance(count, int) and count <= 0:
        return
    eng.wait_ge(sem, count)


def build(nc, x, cT, wmod, wx, win, wout, conv_w, conv_b, A_log, Dvec, w_router, wffn, out):
    with ExitStack() as ctx:
        base = (nc.sbuf_base + 63) // 64 * 64

        def at(name, shape, dt, offset):
            return nc.alloc_sbuf_tensor_at(name, shape, dt, offset=base + offset)

        def sem(name):
            return ctx.enter_context(nc.semaphore(name))

        def psum(name):
            return ctx.enter_context(nc.psum_tensor(name, [P, 512], F32))

        CHB = CH * 512 * 4
        o_raw, o_whi = 0, CHB
        o_wlo = o_whi + 2 * CHB
        o_xs = o_wlo + 2 * CHB
        XSB = KT * ROWS * 4
        o_acc = o_xs + 2 * XSB
        o_a = o_acc + NT * SUB * DM * 4
        o_const = o_a + 5 * HM * TILE * 4
        raw = at("raw", [P, CH, 512], F32, o_raw)
        Whi = at("Whi", [P, 2, CH, 512], F32R, o_whi)
        Wlo = at("Wlo", [P, 2, CH, 512], F32R, o_wlo)
        XShi = at("XShi", [P, KT, ROWS], F32R, o_xs)
        XSlo = at("XSlo", [P, KT, ROWS], F32R, o_xs + XSB)
        acc = at("acc", [P, NT * SUB, DM], F32, o_acc)
        sorted_rows = at("sorted_rows", [P, NT * SUB, DM], F32, o_acc)
        AB = HM * TILE * 4
        ahi = at("ahi", [P, HM, TILE], F32R, o_a)
        alo = at("alo", [P, HM, TILE], F32R, o_a + AB)
        relu_h = at("relu_h", [P, HM, TILE], F32, o_a + 2 * AB)
        twice_h = at("twice_h", [P, HM, TILE], F32, o_a + 3 * AB)
        a_full = at("a_full", [P, HM, TILE], F32, o_a + 4 * AB)
        res_row = [at(f"res_row{s}", [P, ROW], F32, o_raw + s * ROW * 4) for s in range(SUB)]
        out_row = [at(f"out_row{s}", [P, DM], F32, o_raw + SUB * ROW * 4 + s * DM * 4) for s in range(SUB)]

        x_in = at("x_in", [P, 2, TJ, DM], F32, o_whi + CHB)
        z = at("z", [P, TJ, DM], F32, o_wlo + CHB)
        h2 = at("h2", [P, TJ, DM], F32, o_wlo + CHB + TJ * DM * 4)
        cur = [o_xs]

        def take(name, shape, dt=F32):
            o = cur[0]
            cur[0] += (int(np.prod(shape[1:])) * 4 + 31) // 32 * 32
            assert cur[0] <= o_const
            return at(name, shape, dt, o)

        hT = take("hT", [P, 2, KT, L + PAD])
        xc = take("xc", [P, 2, KT, L])
        o_wm = cur[0]
        res = take("res", [P, TJ, ROW])
        yT = take("yT", [P, KT, L])
        wm = at("wm", [P, 3, KT, 512], F32, o_wm)
        u = take("u", [P, L])
        w1 = take("w1", [P, L])
        lw = take("lw", [P, L])
        delta = take("delta", [P, L])
        dA = take("dA", [P, L])
        Bu = take("Bu", [P, L])
        hs = take("hs", [P, L])
        Bs = take("Bs", [P, L])
        Cs = take("Cs", [P, L])
        t2 = take("t2", [P, L])
        bc = take("bc", [P, NB, 3, DM])
        wx_sb = take("wx_sb", [P, KT, 2 * S + 1])
        wdb = take("wdb", [P, KT, P])
        win_sb = take("win_sb", [P, KT, S])
        wout_sb = take("wout_sb", [P, DM])
        gap = take("gap", [P, ROW])
        wr = at("wr", [P, NE, DM], F32, o_wlo + CHB + TJ * DM * 4)
        modrow = at("modrow", [NB, 6, DM], F32, o_raw)

        cur = [o_const]
        top = 229368 - base

        def const(name, shape, dt=F32):
            o = cur[0]
            cur[0] += (int(np.prod(shape[1:])) * 4 + 31) // 32 * 32
            assert cur[0] <= top, cur[0] - top
            return at(name, shape, dt, o)

        ident = const("ident", [P, P])
        before = const("before", [P, P])
        ones = const("ones", [P, P])
        wdiff = const("wdiff", [P, DM])
        c_sb = const("c_sb", [P, KT * NB])
        sc = const("sc", [P, KT * NB])
        sct = const("sct", [P, KT * NB])
        cw = const("cw", [P, KT, TAPS])
        cb = const("cb", [P, KT])
        Dv = const("Dv", [P, KT])
        Al = const("Al", [P, 1])
        Acol = const("Acol", [P, 1])
        cols = const("cols", [P, 3, KT, NB])
        Dga = const("Dga", [P, KT, NB])
        st = const("st", [P, TJ, 6])
        mv = const("mv", [P, TJ, 2])
        ve = const("ve", [P, TJ])
        r0 = const("r0", [P, TJ])
        tt = const("tt", [P, TJ])
        rs = const("rs", [P, TJ])
        nm = const("nm", [P, TJ])
        st2 = const("st2", [P, TJ, 6])
        mv2 = const("mv2", [P, TJ, 2])
        ve2 = const("ve2", [P, TJ])
        r02 = const("r02", [P, TJ])
        tt2 = const("tt2", [P, TJ])
        rs2 = const("rs2", [P, TJ])
        nm2 = const("nm2", [P, TJ])
        lg = const("lg", [P, TJ])
        m1 = const("m1", [P, TJ])
        al = const("al", [P, TJ])
        eal = const("eal", [P, TJ])
        topw = const("topw", [P, TJ])
        incl = const("incl", [P, TJ])
        rank = const("rank", [P, TJ])
        pos = const("pos", [P, TJ])
        run = const("run", [P, 1])
        posI = const("posI", [P, TJ], I32)
        tokI = const("tokI", [P, NB * TJ], I32)
        tokF = const("tokF", [P, NB * TJ])
        back = const("back", [P, NB * TJ])
        n0f = const("n0f", [P, 1])
        n0I = const("n0I", [P, 1], I32)
        gapf = const("gapf", [P, SUB])
        gapI = const("gapI", [P, SUB], I32)
        idx_out = const("idx_out", [P, SUB], I32)

        bank = [psum(f"bank{i}") for i in range(8)]
        pT = bank[0:2]
        pB, pC, pD, pX = bank[2:6]
        pY = bank[6:8]
        hP = bank[0:2]
        yP = bank[2:4]

        mod_dram = nc.dram_tensor("mod_rows", [NB, 3 * DM], F32, kind="Internal").ap()
        rows_dram = nc.dram_tensor("sorted_tokens", [ROWS, DM], F32, kind="Internal").ap()
        res_dram = nc.dram_tensor("sorted_residuals", [ROWS, ROW], F32, kind="Internal").ap()

        s_c = sem("c_landed")
        s_wm = [sem(f"wmod_landed{i}") for i in range(3)]
        s_small = sem("small_landed")
        s_wt = sem("mixer_weights_landed")
        s_wr = sem("router_landed")
        s_bc = sem("mod_broadcast_landed")
        s_md = sem("mod_stored")
        s_x = sem("x_landed")
        s_raw = [sem("raw_fc_landed"), sem("raw_proj_landed")]
        s_xs = [sem(f"sorted_landed{i}") for i in range(NT)]
        s_rr = [sem(f"res_row_landed{i}") for i in range(SUB)]
        s_sc1 = sem("tokens_scattered")
        s_sc2 = sem("residuals_scattered")
        s_out = [sem(f"out_scattered{i}") for i in range(SUB)]
        s_pass = sem("waits_passed")
        s_const = sem("pool_consts")
        s_dconst = sem("dve_consts")
        s_setup = sem("setup_steps")
        s_sil = sem("silu_exp_done")
        s_silu = sem("silu_ready")
        s_mm = sem("mod_chunk_done")
        s_mr = sem("mod_chunk_copied")
        s_mt = sem("mod_columns_done")
        s_cols = sem("mod_columns_ready")
        s_A = sem("A_exp_done")
        s_zz = sem("mixer_stats_ready")
        s_r0 = sem("mixer_rstd_guess")
        s_l0 = sem("mixer_ln_step")
        s_rs = sem("mixer_rstd_ready")
        s_z = sem("z_ready")
        s_zT = sem("zT_done")
        s_hT = sem("hT_ready")
        s_y0 = sem("first_tap_ready")
        s_cv = sem("conv_done")
        s_pd = sem("delta_product_done")
        s_pb = sem("B_C_products_done")
        s_px = sem("state_product_done")
        s_bs = sem("B_C_copied")
        s_u = sem("exp_minus_abs_ready")
        s_ab = sem("abs_ready")
        s_w1 = sem("one_plus_u_ready")
        s_lw = sem("log_ready")
        s_dl = sem("delta_ready")
        s_dA = sem("decay_ready")
        s_bu = sem("Bu_ready")
        s_hm = sem("state_ready")
        s_y = sem("mixer_group_done")
        s_rk = sem("ranks_ready")
        s_t2 = sem("skip_ready")
        s_yT = sem("yT_ready")
        s_x2 = sem("x2_ready")
        s_ve2 = sem("expert_stats_ready")
        s_l2 = sem("expert_ln_step")
        s_r2 = sem("expert_rstd_guess")
        s_rs2 = sem("expert_rstd_ready")
        s_z2 = sem("z2_ready")
        s_h2m = sem("h2_scaled")
        s_h2 = sem("h2_ready")
        s_al = sem("margin_ready")
        s_ea = sem("margin_exp_ready")
        s_tw = sem("top_weight_ready")
        s_gb = sem("gates_ready")
        s_m1 = sem("expert_mask_ready")
        s_pos = sem("positions_ready")
        s_tid = sem("token_numbers_ready")
        s_n0 = sem("count_ready")
        s_va = sem("dve_steps_mixer")
        s_vb = sem("dve_steps_experts")
        s_xt = sem("sorted_transposed")
        s_xhi = sem("sorted_hi_ready")
        s_xlo = sem("sorted_lo_ready")
        s_whi = sem("weights_hi_ready")
        s_wlo = sem("weights_lo_ready")
        s_h = [sem(f"h_done{m}") for m in range(HM)]
        s_relu = [sem(f"relu_ready{m}") for m in range(HM)]
        s_q = [sem(f"twice_h_ready{m}") for m in range(HM)]
        s_sq = [sem(f"a_full_ready{m}") for m in range(HM)]
        s_ah = [sem(f"a_hi_ready{m}") for m in range(HM)]
        s_al2 = [sem(f"a_lo_ready{m}") for m in range(HM)]
        s_yy = [sem(f"y_done{s}") for s in range(SUB)]
        s_au = [sem("a_used0"), s_yy[SUB - 1]]
        s_yu = [sem(f"y_used{s}") for s in range(SUB)]
        s_fin = sem("final_steps")
        s_or = [sem(f"out_row_ready{s}") for s in range(SUB)]

        KA = 8 + 1 + 1 + 3 + 9
        block = ctx.enter_context(nc.Block())

        @block.sync
        def _(sp):
            sp.dma_start(c_sb[:, :], cT).then_inc(s_c, 16)
            sp.dma_start(x_in[:, 0], x[0]).then_inc(s_x, 16)
            for n, ch in enumerate([1, 0, 2]):
                sp.dma_start(wm[:, n], wmod[ch]).then_inc(s_wm[n], 16)
            for dst, src in ((cw[:, :, :], conv_w), (cb[:, :], conv_b), (Dv[:, :], Dvec), (Al[:, :], A_log)):
                sp.dma_start(dst, src).then_inc(s_small, 16)
            for dst, src in ((wx_sb[:, :, :], wx), (win_sb[:, :, :], win), (wout_sb[:, :], wout)):
                sp.dma_start(dst, src).then_inc(s_wt, 16)
            sp.dma_start(wr[:, :, :].rearrange("p e d -> p (e d)"),
                         w_router.rearrange("e d -> (e d)").partition_broadcast(P)).then_inc(s_wr, 16)
            sp.wait_ge(s_x, 16)
            sp.dma_start(x_in[:, 1], x[1]).then_inc(s_x, 16)
            for n, ch in enumerate([4, 3, 5]):
                sp.wait_ge(s_mm, n + 1)
                sp.dma_start(wm[:, n], wmod[ch]).then_inc(s_wm[n], 16)
            sp.wait_ge(s_mr, 6)
            sp.dma_start(mod_dram, modrow[:, 3:6, :].rearrange("b c d -> b (c d)")).then_inc(s_md, 16)
            sp.wait_ge(s_md, 16)
            sp.dma_start(bc[:, :, :, :].rearrange("p b c d -> p (b c d)"),
                         mod_dram.rearrange("b n -> (b n)").partition_broadcast(P)).then_inc(s_bc, 16)
            sp.wait_ge(s_mt, 1)
            for i in range(2):
                sp.dma_start(raw[:, 4 * i:4 * i + 4], wffn[0][:, 4 * i:4 * i + 4]).then_inc(s_raw[i], 16)
            for b in range(2, NB):
                sp.wait_ge(s_x, 16 * b)
                sp.wait_ge(s_x2, TJ * (b - 1))
                sp.dma_start(x_in[:, b % 2], x[b]).then_inc(s_x, 16)
            sp.wait_ge(s_sc1, 16 * (NB * TJ + SUB))
            sp.wait_ge(s_sc2, 16 * (NB * TJ + SUB))
            for t in range(NT):
                sp.dma_start(sorted_rows[:, SUB * t:SUB * t + SUB],
                             rows_dram[TILE * t:TILE * t + TILE].rearrange("(s p) d -> p s d", p=P)).then_inc(s_xs[t], 16)
            with sp.Fori(1, NHB) as hb:
                for i in range(2):
                    sp.wait_ge(s_whi, CH * (hb - 1) + 4 * i + 4)
                    sp.wait_ge(s_wlo, CH * (hb - 1) + 4 * i + 4)
                    sp.dma_start(raw[:, 4 * i:4 * i + 4], wffn[hb, :, 4 * i:4 * i + 4]).then_inc(s_raw[i], 16)
            sp.wait_ge(s_whi, CH * NHB)
            sp.wait_ge(s_wlo, CH * NHB)
            with sp.Fori(0, NT) as t:
                for s in range(SUB):
                    sp.wait_ge(s_or[s], t)
                    sp.dma_start(res_row[s][:, :], res_dram[bass.ds(TILE * t + P * s, P), :]).then_inc(s_rr[s], 16)

        @block.gpsimd
        def _(pool):
            pool.memset(ident[:, :], 0.0).then_inc(s_const, 1)
            pool.memset(before[:, :], 1.0).then_inc(s_const, 1)
            pool.iota(tokI[:, :], pattern=[[P, NB * TJ]], base=0, channel_multiplier=1).then_inc(s_const, 1)
            pool.memset(gap[:, :], 0.0).then_inc(s_const, 1)
            pool.wait_ge(s_const, 4)
            pool.affine_select(out=ident[:, :], in_=ident[:, :], compare_op=ALU.not_equal, fill=1.0, base=0,
                               pattern=[[-1, P]], channel_multiplier=1).then_inc(s_const, 1)
            pool.affine_select(out=before[:, :], in_=before[:, :], compare_op=ALU.is_gt, fill=0.0, base=0,
                               pattern=[[1, P]], channel_multiplier=-1).then_inc(s_const, 1)
            pool.iota(gap[:, 2 * DM:2 * DM + 1].bitcast(I32), pattern=[[0, 1]], base=NO_TOKEN,
                      channel_multiplier=0).then_inc(s_const, 1)
            pool.wait_ge(s_const, 7)

            pool.wait_ge(s_mr, 6)
            pool.memset(res[:, :, 2 * DM:ROW], 0.0).then_inc(s_const, 1)
            pool.wait_ge(s_const, 8)
            pool.wait_ge(s_bc, 16)
            with pool.Fori(0, NB) as b:
                wait(pool, s_sc2, 16 * TJ * b)
                pool.tensor_copy(res[:, :, 2 * DM:2 * DM + 1].bitcast(I32),
                                 tokI[:, bass.ds(TJ * b, TJ)].rearrange("p (j o) -> p j o", o=1)).then_inc(s_tid, 1)
                for j in range(TJ):
                    pool.wait_ge(s_z2, TJ * b + j + 1)
                    pool.sem_inc(s_pass, 1)
                    pool.tensor_tensor(h2[:, j, :], h2[:, j, :], bc[:, b, 0, :], ALU.mult).then_inc(s_h2m, 1)
                pool.wait_ge(s_pos, b + 1)
                pool.wait_ge(s_h2, TJ * (b + 1))
                pool.sem_inc(s_pass, 1)
                for j in range(TJ):
                    pool.indirect_dma_start(out=rows_dram, out_offset=bass.IndirectOffsetOnAxis(ap=posI[:, j:j + 1], axis=0),
                                            in_=h2[:, j, :], in_offset=None).then_inc(s_sc1, 16)
                pool.wait_ge(s_gb, TJ * (b + 1))
                pool.wait_ge(s_tid, b + 1)
                pool.sem_inc(s_pass, 1)
                for j in range(TJ):
                    pool.indirect_dma_start(out=res_dram, out_offset=bass.IndirectOffsetOnAxis(ap=posI[:, j:j + 1], axis=0),
                                            in_=res[:, j, :], in_offset=None).then_inc(s_sc2, 16)
            pool.wait_ge(s_n0, 2)
            for g in range(SUB):
                pool.indirect_dma_start(out=rows_dram, out_offset=bass.IndirectOffsetOnAxis(ap=gapI[:, g:g + 1], axis=0),
                                        in_=gap[:, 0:DM], in_offset=None).then_inc(s_sc1, 16)
                pool.indirect_dma_start(out=res_dram, out_offset=bass.IndirectOffsetOnAxis(ap=gapI[:, g:g + 1], axis=0),
                                        in_=gap[:, :], in_offset=None).then_inc(s_sc2, 16)

            def low(hb, c):
                pool.wait_ge(s_whi, CH * hb + c + 1)
                pool.tensor_tensor(Wlo[:, hb % 2, c, :], raw[:, c, :], Whi[:, hb % 2, c, :].bitcast(F32),
                                   ALU.subtract).then_inc(s_wlo, 1)

            for c in range(CH):
                low(0, c)
            with pool.Fori(1, NHB) as hb:
                with pool.Fori(0, CH) as c:
                    low(hb, c)
            with pool.Fori(0, NT) as t:
                for s in range(SUB):
                    pool.wait_ge(s_or[s], t + 1)
                    pool.sem_inc(s_pass, 1)
                    pool.indirect_dma_start(out=out, out_offset=bass.IndirectOffsetOnAxis(ap=idx_out[:, s:s + 1], axis=0),
                                            in_=out_row[s][:, :], in_offset=None, bounds_check=TOK - 1,
                                            oob_is_err=False).then_inc(s_out[s], 16)
            for s in range(SUB):
                pool.wait_ge(s_out[s], 16 * NT)

        @block.scalar
        def _(act):
            act.preload_act_table_set("natural_log_exp_and_others")
            act.wait_ge(s_c, 16)
            act.activation(sc[:, :], c_sb[:, :], ACT.Exp, scale=-1.0).then_inc(s_sil, 1)
            act.wait_ge(s_small, 64)
            act.activation(Acol[:, :], Al[:, :], ACT.Exp).then_inc(s_A, 1)

            def norm1(b):
                act.wait_ge(s_zz, b + 1)
                act.activation(tt[:, :], ve[:, :], ACT.Ln).then_inc(s_l0, 1)
                act.wait_ge(s_l0, b + 1)
                act.activation(r0[:, :], tt[:, :], ACT.Exp, scale=-0.5).then_inc(s_r0, 1)
                act.wait_ge(s_rs, b + 1)
                wait(act, s_zT, KT * b)
                for j in range(TJ):
                    act.activation(z[:, j, :], x_in[:, b % 2, j, :], ACT.Identity, bias=nm[:, j:j + 1],
                                   scale=rs[:, j:j + 1]).then_inc(s_z, 1)

            def modulate1(b):
                wait(act, s_cv, KT * (b - 1))
                wait(act, s_px, b - 1)
                for k in range(KT):
                    act.wait_ge(s_zT, KT * b + k + 1)
                    act.activation(hT[:, b % 2, k, PAD:PAD + L], pT[k % 2][:, :], ACT.Identity,
                                   bias=cols[:, 0, k, bass.ds(b, 1)], scale=cols[:, 1, k, bass.ds(b, 1)]).then_inc(s_hT, 1)
                for k in range(KT):
                    act.wait_ge(s_hT, KT * b + k + 1)
                    act.activation(xc[:, b % 2, k, :], hT[:, b % 2, k, PAD:PAD + L], ACT.Identity,
                                   bias=cb[:, k:k + 1], scale=cw[:, k, PAD:TAPS]).then_inc(s_y0, 1)

            def copy_BC(b):
                wait(act, s_hm, b)
                act.wait_ge(s_pb, 2 * b + 1)
                act.copy(Bs[:, :], pB[:, :]).then_inc(s_bs, 1)
                act.wait_ge(s_pb, 2 * b + 2)
                act.copy(Cs[:, :], pC[:, :]).then_inc(s_bs, 1)

            def decay(b):
                act.wait_ge(s_pd, b + 1)
                wait(act, s_dl, b)
                act.activation(u[:, :], pD[:, :], ACT.Abs).then_inc(s_ab, 1)
                act.wait_ge(s_ab, b + 1)
                act.activation(u[:, :], u[:, :], ACT.Exp, scale=-1.0).then_inc(s_u, 1)
                act.wait_ge(s_w1, b + 1)
                act.activation(lw[:, :], w1[:, :], ACT.Ln).then_inc(s_lw, 1)
                act.wait_ge(s_dl, b + 1)
                wait(act, s_hm, b)
                act.activation(dA[:, :], delta[:, :], ACT.Exp, scale=Acol[:, 0:1]).then_inc(s_dA, 1)

            def skip(b):
                for m in range(KT):
                    wait(act, s_yT, KT * b + m)
                    act.activation(t2[:, :], xc[:, b % 2, m, :], ACT.Identity,
                                   scale=Dga[:, m, bass.ds(b, 1)]).then_inc(s_t2, 1)

            def norm2(b):
                act.wait_ge(s_ve2, b + 1)
                act.activation(tt2[:, :], ve2[:, :], ACT.Ln).then_inc(s_l2, 1)
                act.wait_ge(s_l2, b + 1)
                act.activation(r02[:, :], tt2[:, :], ACT.Exp, scale=-0.5).then_inc(s_r2, 1)
                act.wait_ge(s_rs2, b + 1)
                wait(act, s_sc1, 16 * TJ * b)
                for j in range(TJ):
                    act.activation(h2[:, j, :], res[:, j, 0:DM], ACT.Identity, bias=nm2[:, j:j + 1],
                                   scale=rs2[:, j:j + 1]).then_inc(s_z2, 1)

            def gates(b):
                act.wait_ge(s_al, b + 1)
                act.activation(eal[:, :], al[:, :], ACT.Exp, scale=-1.0).then_inc(s_ea, 1)
                act.wait_ge(s_tw, b + 1)
                for j in range(TJ):
                    act.activation(res[:, j, DM:2 * DM], bc[:, b, 2, :], ACT.Identity,
                                   scale=topw[:, j:j + 1]).then_inc(s_gb, 1)

            norm1(0)
            act.wait_ge(s_cols, KT)
            modulate1(0)
            copy_BC(0)
            act.wait_ge(s_bc, 16)
            with act.Fori(0, NB - 1) as b:
                norm1(b + 1)
                modulate1(b + 1)
                decay(b)
                copy_BC(b + 1)
                skip(b)
                norm2(b)
                gates(b)
            decay(NB - 1)
            skip(NB - 1)
            norm2(NB - 1)
            gates(NB - 1)

            def split(hb, c):
                act.activation(Whi[:, hb % 2, c, :], raw[:, c, :], ACT.Copy).then_inc(s_whi, 1)

            for i in range(2):
                act.wait_ge(s_raw[i], 16)
                for c in range(4 * i, 4 * i + 4):
                    split(0, c)
            for s in range(NT * SUB):
                act.wait_ge(s_xt, s + 1)
                act.activation(XShi[:, :, P * s:P * s + P], pY[s % 2][:, :].rearrange("p (k t) -> p k t", k=KT),
                               ACT.Copy).then_inc(s_xhi, 1)

            def job(hb, t):
                i = NT * hb + t
                for m in range(HM):
                    act.wait_ge(s_h[m], i + 1)
                    wait(act, s_q[m], i)
                    act.activation(relu_h[:, m, :], hP[m][:, 0:TILE], ACT.Relu).then_inc(s_relu[m], 1)
                for m in range(HM):
                    act.wait_ge(s_q[m], i + 1)
                    wait(act, s_al2[m], i)
                    act.activation(a_full[:, m, :], twice_h[:, m, :], ACT.Square, scale=0.5).then_inc(s_sq[m], 1)
                    wait(act, s_au[m], i)
                    act.activation(ahi[:, m, :], twice_h[:, m, :], ACT.Square, scale=0.5).then_inc(s_ah[m], 1)

            with act.Fori(0, NHB - 1) as hb:
                job(hb, 0)
                act.wait_ge(s_yy[SUB - 1], NT * hb)
                for i in range(2):
                    with act.Fori(4 * i, 4 * i + 4) as c:
                        job(hb, c + 1)
                        act.wait_ge(s_raw[i], 16 * (hb + 2))
                        split(hb + 1, c)
            with act.Fori(0, NT) as t:
                job(NHB - 1, t)

        @block.tensor
        def _(pe):
            pe.wait_ge(s_const, 7)
            pe.wait_ge(s_silu, 1)
            def modulation(n):
                if n >= 2:
                    pe.wait_ge(s_mr, n - 1)
                pe.wait_ge(s_wm[n % 3], 16 * (n // 3 + 1))
                for k in range(KT):
                    mm = pe.matmul(pY[n % 2][0:NB, :], sc[:, NB * k:NB * k + NB], wm[:, n % 3, k, :],
                                   start=(k == 0), stop=(k == KT - 1))
                mm.then_inc(s_mm, 1)

            for n in range(3):
                modulation(n)
            pe.wait_ge(s_mr, 3)
            for n in range(3):
                for k in range(KT):
                    o = NB * (KT * n + k)
                    mm = pe.transpose(pX[:, o:o + NB], modrow[0:NB, n, P * k:P * k + P], ident[0:NB, 0:NB])
            mm.then_inc(s_mt, 1)

            def transposes1(b):
                pe.wait_ge(s_z, TJ * (b + 1))
                for k in range(KT):
                    wait(pe, s_hT, KT * b + k - 1)
                    for j in range(TJ):
                        mm = pe.transpose(pT[k % 2][:, P * j:P * j + P], z[:, j, P * k:P * k + P], ident[:, :])
                    mm.then_inc(s_zT, 1)

            def products(b):
                pe.wait_ge(s_hT, KT * (b + 1))
                wait(pe, s_dl, b)
                for k in range(KT):
                    mm = pe.matmul(pD[:, :], wdb[:, k, :], hT[:, b % 2, k, PAD:PAD + L], start=(k == 0), stop=(k == KT - 1))
                mm.then_inc(s_pd, 1)
                wait(pe, s_bs, 2 * b)
                for n, bk in enumerate((pB, pC)):
                    for k in range(KT):
                        mm = pe.matmul(bk[:, :], wx_sb[:, k, S * n:S * n + S], hT[:, b % 2, k, PAD:PAD + L],
                                       start=(k == 0), stop=(k == KT - 1))
                    mm.then_inc(s_pb, 1)
                pe.wait_ge(s_cv, KT * (b + 1))
                wait(pe, s_bu, b)
                for k in range(KT):
                    mm = pe.matmul(pX[:, :], win_sb[:, k, :], xc[:, b % 2, k, :], start=(k == 0), stop=(k == KT - 1))
                mm.then_inc(s_px, 1)

            def mix(b):
                pe.wait_ge(s_hm, b + 1)
                for m in range(KT):
                    if m < 2:
                        wait(pe, s_rk, b)
                    else:
                        pe.wait_ge(s_yT, KT * b + m - 1)
                    pe.matmul(pY[m % 2][:, :], wout_sb[:, P * m:P * m + P], hs[:, :], start=True, stop=True).then_inc(s_y, 1)
                pe.wait_ge(s_yT, KT * (b + 1))
                for j in range(TJ):
                    if j >= 2:
                        pe.wait_ge(s_x2, TJ * b + j - 1)
                    for m in range(KT):
                        mm = pe.transpose(pY[j % 2][:, P * m:P * m + P], yT[:, m, P * j:P * j + P], ident[:, :])
                    mm.then_inc(s_y, 1)
                pe.wait_ge(s_m1, b + 1)
                pe.wait_ge(s_x2, TJ * (b + 1))
                pe.matmul(pY[0][:, 0:TJ], before[:, :], m1[:, :], start=True, stop=True).then_inc(s_y, 1)
                pe.matmul(pY[1][:, 0:TJ], ones[:, :], m1[:, :], start=True, stop=True).then_inc(s_y, 1)

            pe.wait_ge(s_dconst, 1)
            transposes1(0)
            pe.wait_ge(s_cols, KT)
            products(0)
            for n in range(3, 6):
                modulation(n)
            pe.wait_ge(s_mr, 6)
            with pe.Fori(0, NB - 1) as b:
                transposes1(b + 1)
                products(b + 1)
                mix(b)
            mix(NB - 1)

            pe.wait_ge(s_rk, NB)
            for s in range(NT * SUB):
                pe.wait_ge(s_xs[s // SUB], 16)
                wait(pe, s_xhi, s - 1)
                wait(pe, s_xlo, s - 1)
                for k in range(KT):
                    mm = pe.transpose(pY[s % 2][:, P * k:P * k + P], sorted_rows[:, s, P * k:P * k + P], ident[:, :])
                mm.then_inc(s_xt, 1)
            pe.wait_ge(s_n0, 2)
            n0 = pe.value_load(n0I[0:1, 0:1], min_val=0, max_val=TOK)
            pe.wait_ge(s_xhi, NT * SUB)
            pe.wait_ge(s_xlo, NT * SUB)
            PARTS = ((0, 0), (0, 1), (1, 0))
            W, XS, A = (Whi, Wlo), (XShi, XSlo), (ahi, alo)

            def fc(par, hb, t):
                i = NT * hb + t

                def body(e):
                    for m in range(HM):
                        n = 0
                        for k in range(KT):
                            for wp, xp in PARTS:
                                o = HB * (k % 2) + P * m
                                mm = pe.matmul(hP[m][:, 0:TILE], W[wp][:, par, 2 * e + k // 2, o:o + P],
                                               XS[xp][:, k, bass.ds(t * TILE, TILE)],
                                               start=(n == 0), stop=(n == 3 * KT - 1))
                                n += 1
                        mm.then_inc(s_h[m], 1)

                for m in range(HM):
                    wait(pe, s_q[m], i)
                with pe.If(t * TILE < n0):
                    body(0)
                with pe.Else():
                    body(1)

            def proj(par, hb, t):
                i = NT * hb + t

                def body(e):
                    for m in range(HM):
                        for s in range(SUB):
                            for n, (ap, wp) in enumerate(PARTS):
                                mm = pe.matmul(yP[s][:, :], A[ap][:, m, P * s:P * s + P], W[wp][:, par, 4 + 2 * e + m, :],
                                               start=(m == 0 and n == 0), stop=(m == HM - 1 and n == 2))
                            if m == HM - 1:
                                mm.then_inc(s_yy[s], 1)
                        if m < HM - 1:
                            mm.then_inc(s_au[m], 1)

                for m in range(HM):
                    pe.wait_ge(s_al2[m], i + 1)
                for s in range(SUB):
                    wait(pe, s_yu[s], i)
                with pe.If(t * TILE < n0):
                    body(0)
                with pe.Else():
                    body(1)

            def block_ready(hb):
                pe.wait_ge(s_whi, CH * (hb + 1))
                pe.wait_ge(s_wlo, CH * (hb + 1))

            block_ready(0)
            fc(0, 0, 0)
            with pe.Fori(0, NHB // 2) as pair:
                for par in range(2):
                    hb = 2 * pair + par
                    with pe.Fori(1, NT) as t:
                        fc(par, hb, t)
                        proj(par, hb, t - 1)
                    if par == 0:
                        block_ready(hb + 1)
                        fc(1, hb + 1, 0)
                    else:
                        with pe.If(pair < NHB // 2 - 1):
                            block_ready(hb + 1)
                            fc(0, hb + 1, 0)
                    proj(par, hb, NT - 1)

        @block.vector
        def _(dve):
            dve.memset(ones[:, :], 1.0).then_inc(s_setup, 1)
            dve.memset(run[:, :], 0.0).then_inc(s_setup, 1)
            dve.memset(hT[:, :, :, 0:PAD], 0.0).then_inc(s_dconst, 1)
            su = Steps(dve, s_setup, 2)
            dve.wait_ge(s_sil, 1)
            su.link(dve.tensor_scalar(sct[:, :], sc[:, :], 1.0, None, ALU.add))
            su.link(dve.reciprocal(sct[:, :], sct[:, :]))
            dve.tensor_tensor(sc[:, :], c_sb[:, :], sct[:, :], ALU.mult).then_inc(s_silu, 1)

            def stats(xs, rows, stt, mvt, vet, done):
                for j in range(TJ):
                    xs.mark(dve.bn_stats(stt[:, j, :], rows(j)))
                xs.settle()
                dve.sem_inc(s_pass, 1)
                for j in range(TJ):
                    xs.mark(dve.bn_aggr(mvt[:, j, :], stt[:, j, :]))
                xs.settle()
                dve.tensor_scalar(vet[:, :], mvt[:, :, 1], EPS, None, ALU.add).then_inc(done, 1)

            def newton(xs, vet, guess, tmp, rst, mvt, nmt, ready):
                xs.link(dve.tensor_tensor(tmp[:, :], guess[:, :], guess[:, :], ALU.mult))
                xs.link(dve.tensor_tensor(tmp[:, :], tmp[:, :], vet[:, :], ALU.mult))
                xs.link(dve.tensor_scalar(tmp[:, :], tmp[:, :], -0.5, 1.5, ALU.mult, ALU.add))
                xs.link(dve.tensor_tensor(rst[:, :], guess[:, :], tmp[:, :], ALU.mult))
                dve.scalar_tensor_tensor(nmt[:, :], mvt[:, :, 0], -1.0, rst[:, :], ALU.mult, ALU.mult).then_inc(ready, 1)

            PROJECT_STEPS = 2 * TJ + 4 + (PAD - 1) * KT

            def project(b):
                xs = Steps(dve, s_va, PROJECT_STEPS * b)
                dve.wait_ge(s_x, 16 * (b + 1))
                wait(dve, s_z, TJ * b)
                stats(xs, lambda j: x_in[:, b % 2, j, :], st, mv, ve, s_zz)
                dve.wait_ge(s_r0, b + 1)
                newton(xs, ve, r0, tt, rs, mv, nm, s_rs)
                if isinstance(b, int) and b == 0:
                    setup()
                    modulation_rows(0)
                for tap in range(PAD):
                    for k in range(KT):
                        if tap == 0:
                            dve.wait_ge(s_y0, KT * b + k + 1)
                        else:
                            n = 2 * TJ + 4 + KT * (tap - 1) + k + 1
                            dve.wait_ge(s_va, xs.base + n)
                        ins = dve.scalar_tensor_tensor(xc[:, b % 2, k, :], hT[:, b % 2, k, tap:tap + L],
                                                       cw[:, k, tap:tap + 1], xc[:, b % 2, k, :], ALU.mult, ALU.add)
                        if tap < PAD - 1:
                            xs.mark(ins)
                        else:
                            ins.then_inc(s_cv, 1)
                assert xs.n == PROJECT_STEPS
                if isinstance(b, int) and b == 0:
                    modulation_rows(1)

            def setup():
                dve.wait_ge(s_wt, 48)
                for k in range(KT):
                    su.mark(dve.tensor_scalar(wdb[:, k, :], ones[:, :], wx_sb[:, k, 2 * S:2 * S + 1], None, ALU.mult))
                dve.wait_ge(s_wr, 16)
                su.mark(dve.tensor_tensor(wdiff[:, :], wr[:, 1, :], wr[:, 0, :], ALU.subtract))
                dve.wait_ge(s_const, 7)
                su.link(dve.tensor_copy(tokF[:, :], tokI[:, :]))
                su.mark(dve.tensor_scalar(back[:, :], tokF[:, :], -1.0, float(ROWS - 1), ALU.mult, ALU.add))
                dve.wait_ge(s_A, 1)
                su.mark(dve.tensor_scalar(Acol[:, :], Acol[:, :], -1.0, None, ALU.mult))

            def modulation_rows(half):
                for n, row in list(enumerate((1, 0, 2, 4, 3, 5)))[3 * half:3 * half + 3]:
                    dve.wait_ge(s_mm, n + 1)
                    one = 1.0 if row in (1, 4) else 0.0
                    dst = {3: 4, 4: 3}.get(row, row)
                    ins = dve.tensor_scalar(modrow[0:NB, dst, :], pY[n % 2][0:NB, :], one, None, ALU.add)
                    if row not in (2, 5):
                        ins.then_inc(s_mr, 1)
                    else:
                        su.link(ins)
                        g = modrow[0:NB, row, :]
                        sg, ab = u[0:NB, :], w1[0:NB, :]
                        su.link(dve.tensor_scalar(sg, g, 0.0, 2.0, ALU.is_ge, ALU.mult))
                        su.link(dve.scalar_tensor_tensor(ab, g, -1.0, g, ALU.mult, ALU.max))
                        su.link(dve.tensor_scalar(ab, ab, 0.25, None, ALU.max))
                        dve.scalar_tensor_tensor(g, sg, -1.0, ab, ALU.add, ALU.mult).then_inc(s_mr, 1)
                    if n == 2:
                        dve.wait_ge(s_mt, 1)
                        su.link(dve.tensor_copy(cols[:, :, :, :].rearrange("p n k b -> p (n k b)"), pX[:, 0:3 * KT * NB]))
                        for k in range(KT):
                            dve.tensor_scalar(Dga[:, k, :], cols[:, 2, k, :], Dv[:, k:k + 1], None, ALU.mult).then_inc(s_cols, 1)

            KB = 3 + 3 * 0
            def mix(b):
                xs = Steps(dve, s_vb, MIX_STEPS * b)
                dve.wait_ge(s_u, b + 1)
                wait(dve, s_lw, b)
                dve.tensor_scalar(w1[:, :], u[:, :], 1.0, None, ALU.add).then_inc(s_w1, 1)
                dve.wait_ge(s_w1, b + 1)
                xs.link(dve.scalar_tensor_tensor(u[:, :], w1[:, :], -1.0, u[:, :], ALU.add, ALU.subtract))
                dve.wait_ge(s_lw, b + 1)
                xs.link(dve.tensor_tensor(lw[:, :], lw[:, :], u[:, :], ALU.subtract))
                wait(dve, s_dA, b)
                dve.scalar_tensor_tensor(delta[:, :], pD[:, :], 0.0, lw[:, :], ALU.max, ALU.add).then_inc(s_dl, 1)
                dve.wait_ge(s_dl, b + 1)
                dve.wait_ge(s_bs, 2 * b + 2)
                xs.link(dve.tensor_tensor(Bu[:, :], delta[:, :], Bs[:, :], ALU.mult))
                dve.wait_ge(s_px, b + 1)
                dve.tensor_tensor(Bu[:, :], Bu[:, :], pX[:, :], ALU.mult).then_inc(s_bu, 1)
                dve.wait_ge(s_bu, b + 1)
                dve.wait_ge(s_dA, b + 1)
                wait(dve, s_y, (2 * KT + 2) * b)
                xs.link(dve.tensor_tensor_scan(hs[:, :], dA[:, :], Bu[:, :], 0.0, ALU.mult, ALU.add))
                dve.tensor_tensor(hs[:, :], hs[:, :], Cs[:, :], ALU.mult).then_inc(s_hm, 1)
                G = 2 * KT + 2
                for m in range(KT):
                    dve.wait_ge(s_y, G * b + m + 1)
                    dve.wait_ge(s_t2, KT * b + m + 1)
                    dve.scalar_tensor_tensor(yT[:, m, :], pY[m % 2][:, :], cols[:, 2, m, bass.ds(b, 1)], t2[:, :],
                                             ALU.mult, ALU.add).then_inc(s_yT, 1)
                wait(dve, s_sc2, 16 * TJ * b)
                for j in range(TJ):
                    dve.wait_ge(s_y, G * b + KT + j + 1)
                    dve.tensor_tensor(res[:, j, 0:DM], pY[j % 2][:, :], x_in[:, b % 2, j, :], ALU.add).then_inc(s_x2, 1)
                dve.wait_ge(s_x2, TJ * (b + 1))
                stats(xs, lambda j: res[:, j, 0:DM], st2, mv2, ve2, s_ve2)
                dve.wait_ge(s_r2, b + 1)
                newton(xs, ve2, r02, tt2, rs2, mv2, nm2, s_rs2)
                for j in range(TJ):
                    dve.wait_ge(s_h2m, TJ * b + j + 1)
                    dve.tensor_tensor(h2[:, j, :], h2[:, j, :], bc[:, b, 1, :], ALU.add).then_inc(s_h2, 1)
                for j in range(TJ):
                    dve.wait_ge(s_h2, TJ * b + j + 1)
                    xs.mark(dve.tensor_tensor_reduce(yT[:, j, :], h2[:, j, :], wdiff[:, :], 1.0, 0.0, ALU.mult, ALU.add,
                                                     lg[:, j:j + 1]))
                xs.settle()
                dve.tensor_scalar(m1[:, :], lg[:, :], 0.0, None, ALU.is_gt).then_inc(s_m1, 1)
                dve.scalar_tensor_tensor(al[:, :], lg[:, :], -1.0, lg[:, :], ALU.mult, ALU.max).then_inc(s_al, 1)
                dve.wait_ge(s_m1, b + 1)
                dve.wait_ge(s_y, G * b + 2 * KT + 2)
                xs.link(dve.tensor_tensor_scan(incl[:, :], ones[:, 0:TJ], pY[1][:, 0:TJ], run[:, 0:1], ALU.mult, ALU.add))
                xs.link(dve.tensor_copy(run[:, :], incl[:, TJ - 1:TJ]))
                xs.link(dve.tensor_tensor(rank[:, :], incl[:, :], pY[1][:, 0:TJ], ALU.subtract))
                dve.tensor_tensor(rank[:, :], rank[:, :], pY[0][:, 0:TJ], ALU.add).then_inc(s_rk, 1)
                dve.wait_ge(s_rk, b + 1)
                xs.link(dve.tensor_tensor(pos[:, :], m1[:, :], back[:, bass.ds(TJ * b, TJ)], ALU.mult))
                xs.link(dve.tensor_tensor(pos[:, :], pos[:, :], tokF[:, bass.ds(TJ * b, TJ)], ALU.add))
                wait(dve, s_sc1, 16 * TJ * b)
                dve.tensor_tensor(posI[:, :], pos[:, :], rank[:, :], ALU.subtract).then_inc(s_pos, 1)
                dve.wait_ge(s_ea, b + 1)
                xs.link(dve.tensor_scalar(topw[:, :], eal[:, :], 1.0, None, ALU.add))
                dve.reciprocal(topw[:, :], topw[:, :]).then_inc(s_tw, 1)
                assert xs.n == MIX_STEPS, xs.n

            MIX_STEPS = 4 + 2 * TJ + 4 + TJ + 3 + 2 + 1
            project(0)
            with dve.Fori(0, NB - 1) as b:
                project(b + 1)
                mix(b)
            mix(NB - 1)

            fs = Steps(dve, s_fin, 0)
            fs.link(dve.tensor_scalar(n0f[:, :], run[:, :], -1.0, float(TOK), ALU.mult, ALU.add))
            dve.tensor_copy(n0I[:, :], n0f[:, :]).then_inc(s_n0, 1)
            fs.link(dve.tensor_scalar(gapf[:, :], tokF[:, 0:SUB], n0f[:, 0:1], None, ALU.add))
            dve.tensor_copy(gapI[:, :], gapf[:, :]).then_inc(s_n0, 1)

            for s in range(NT * SUB):
                dve.wait_ge(s_xhi, s + 1)
                dve.tensor_tensor(XSlo[:, :, P * s:P * s + P], pY[s % 2][:, :].rearrange("p (k t) -> p k t", k=KT),
                                  XShi[:, :, P * s:P * s + P].bitcast(F32), ALU.subtract).then_inc(s_xlo, 1)

            def twice(hb, t):
                i = NT * hb + t
                for m in range(HM):
                    dve.wait_ge(s_relu[m], i + 1)
                    wait(dve, s_ah[m], i)
                    dve.tensor_tensor(twice_h[:, m, :], relu_h[:, m, :], hP[m][:, 0:TILE], ALU.add).then_inc(s_q[m], 1)

            def low(hb, t):
                i = NT * hb + t
                for m in range(HM):
                    dve.wait_ge(s_ah[m], i + 1)
                    dve.tensor_tensor(alo[:, m, :], a_full[:, m, :], ahi[:, m, :].bitcast(F32),
                                      ALU.subtract).then_inc(s_al2[m], 1)

            def accumulate(mode, hb, t):
                i = NT * hb + t
                for s in range(SUB):
                    dve.wait_ge(s_yy[s], i + 1)
                    sub = acc[:, bass.ds(SUB * t + s, 1), :].rearrange("p o d -> p (o d)")
                    if mode == "first":
                        dve.tensor_copy(sub, yP[s][:, :]).then_inc(s_yu[s], 1)
                    elif mode == "add":
                        dve.tensor_tensor(sub, sub, yP[s][:, :], ALU.add).then_inc(s_yu[s], 1)
                    else:
                        dve.tensor_tensor(sub, sub, yP[s][:, :], ALU.add).then_inc(s_yu[s], 1)
                        dve.wait_ge(s_yu[s], i + 1)
                        dve.wait_ge(s_rr[s], 16 * (t + 1))
                        wait(dve, s_out[s], 16 * t)
                        dve.tensor_tensor(sub, sub, res_row[s][:, DM:2 * DM], ALU.mult).then_inc(s_fin, 1)
                        dve.tensor_copy(idx_out[:, s:s + 1], res_row[s][:, 2 * DM:2 * DM + 1].bitcast(I32)).then_inc(s_fin, 1)
                        dve.wait_ge(s_fin, 2 + 2 * (SUB * t + s + 1))
                        dve.tensor_tensor(out_row[s][:, :], sub, res_row[s][:, 0:DM], ALU.add).then_inc(s_or[s], 1)

            def blocks(prev, mode, hb):
                twice(hb, 0)
                if prev:
                    accumulate(prev, hb - 1, NT - 1)
                low(hb, 0)
                with dve.Fori(1, NT) as t:
                    twice(hb, t)
                    accumulate(mode, hb, t - 1)
                    low(hb, t)

            blocks(None, "first", 0)
            blocks("first", "add", 1)
            with dve.Fori(2, NHB - 1) as hb:
                blocks("add", "add", hb)
            blocks("add", "last", NHB - 1)
            accumulate("last", NHB - 1, NT - 1)


def kernel(**inputs):
    import concourse.bacc as bacc
    from concourse.bass_utils import run_bass_kernel_spmd as run_spmd

    a = {k.removeprefix("L0_"): np.asarray(v) for k, v in inputs.items()}

    def rows(m):
        return m.reshape(m.shape[0] // P, P, -1).transpose(1, 0, 2)

    fc = a["ffn_w_fc"].reshape(NE, NHB, HB, KT, P).transpose(1, 4, 0, 3, 2).reshape(NHB, P, CH // 2, 512)
    proj = a["ffn_w_proj"].reshape(NE, DM, NHB, HM, P).transpose(2, 4, 0, 3, 1).reshape(NHB, P, CH // 2, 512)
    arrays = {
        "x": a["attn_x"].reshape(NB, TJ, P, DM).transpose(0, 2, 1, 3),
        "cT": rows(a["c"].T).reshape(P, KT * NB),
        "wmod": a["wmod"].reshape(KT, P, 6, DM).transpose(2, 1, 0, 3),
        "wx": rows(a["attn_Wxproj"].T),
        "win": rows(a["attn_Winproj"].T),
        "wout": a["attn_Woutproj"].T,
        "conv_w": rows(a["attn_conv_w"].reshape(DM, TAPS)),
        "conv_b": a["attn_conv_b"].reshape(KT, P).T,
        "A_log": a["attn_A_log"].reshape(S, 1),
        "Dvec": a["attn_D"].reshape(KT, P).T,
        "w_router": a["ffn_w_router"],
        "wffn": np.concatenate([fc, proj], axis=2),
    }
    arrays = {k: np.ascontiguousarray(v) for k, v in arrays.items()}
    nc = bacc.Bacc("TRN2", target_bir_lowering=False, num_devices=1)
    args = [nc.dram_tensor(k, v.shape, mybir.dt.from_np(v.dtype), kind="ExternalInput").ap() for k, v in arrays.items()]
    out = nc.dram_tensor("out", (TOK, DM), F32, kind="ExternalOutput").ap()
    build(nc, *args, out)
    r = run_spmd(nc, [arrays], core_ids=[0])
    return r.results[0]["out"].reshape(NB, L, DM)
```

```python
import concourse.bass as bass
from concourse import mybir
import numpy as np
from contextlib import ExitStack

F32 = mybir.dt.float32
F32R = mybir.dt.float32r
I32 = mybir.dt.int32
U32 = mybir.dt.uint32
ALU = mybir.AluOpType
ACT = mybir.ActivationFunctionType

P = 128
NB = 4
L = 512
DM = 512
S = 128
TAPS = 4
PAD = TAPS - 1
HID = 2048
NE = 2
TOK = NB * L
KT = DM // P
TJ = L // P
TILE = 256
SUB = TILE // P
NT = TOK // TILE + 1
ROWS = NT * TILE
HB = 256
NHB = HID // HB
HM = HB // P
CH = 8
ROW = DM + 8
XRING = 3
FIRST = 2
RING = 4
MODW = 3 * DM + 8
EPS = 1e-5
NO_TOKEN = 2 * TOK - 1


class Steps:

    def __init__(self, eng, sem):
        self.eng, self.sem, self.n = eng, sem, 0

    def mark(self, ins):
        ins.then_inc(self.sem, 1)
        self.n += 1
        return self.n

    def settle(self):
        self.eng.wait_ge(self.sem, self.n)

    def link(self, ins):
        self.mark(ins)
        self.settle()


def wait(eng, sem, count):
    if isinstance(count, int) and count <= 0:
        return
    eng.wait_ge(sem, count)


def build(nc, x, cT, wmod, wx, win, wout, conv_w, conv_b, A_log, Dvec, w_router, wffn, out):
    with ExitStack() as ctx:
        base = (nc.sbuf_base + 63) // 64 * 64

        def at(name, shape, dt, offset):
            return nc.alloc_sbuf_tensor_at(name, shape, dt, offset=base + offset)

        def sem(name):
            return ctx.enter_context(nc.semaphore(name))

        def psum(name):
            return ctx.enter_context(nc.psum_tensor(name, [P, 512], F32))

        CHB = CH * 512 * 4
        o_raw, o_whi = 0, CHB
        o_wlo = o_whi + CHB + 2 * TJ * ROW * 4
        o_xs = o_wlo + 2 * CHB
        XSB = KT * ROWS * 4
        o_acc = o_xs + 2 * XSB
        AB = HM * TILE * 4
        o_a = o_acc + NT * SUB * DM * 4
        o_const = o_a + 5 * AB
        raw = at("raw", [P, CH, 512], F32, o_raw)
        Whi = at("Whi", [P, 2, CH, 512], F32R, o_whi)
        Wlo = at("Wlo", [P, 2, CH, 512], F32R, o_wlo)
        XShi = at("XShi", [P, KT, ROWS], F32R, o_xs)
        XSlo = at("XSlo", [P, KT, ROWS], F32R, o_xs + XSB)
        acc = at("acc", [P, NT * SUB, DM], F32, o_acc)
        sorted_rows = at("sorted_rows", [P, NT * SUB, DM], F32, o_acc)
        alo = at("alo", [P, HM, TILE], F32R, o_a)
        ahi = at("ahi", [P, HM, TILE], F32R, o_a + AB)
        relu_h = at("relu_h", [P, HM, TILE], F32, o_a + 2 * AB)
        twice_h = at("twice_h", [P, HM, TILE], F32, o_a + 3 * AB)
        a_full = at("a_full", [P, HM, TILE], F32, o_a + 4 * AB)
        res_row = [[at(f"res_row{o}_{s}", [P, ROW], F32, o_raw + (SUB * o + s) * ROW * 4) for s in range(SUB)] for o in range(RING)]
        gb_row = [[at(f"gb_row{o}_{s}", [P, DM], F32, o_wlo + (SUB * o + s) * DM * 4) for s in range(SUB)] for o in range(RING)]

        res = at("res", [P, 2, TJ, ROW], F32, o_whi + CHB)
        z = at("z", [P, TJ, DM], F32, o_wlo + CHB)
        h2 = at("h2", [P, TJ, DM], F32, o_wlo + CHB + TJ * DM * 4)
        cur = [o_xs]

        def take(name, shape, dt=F32):
            o = cur[0]
            cur[0] += (int(np.prod(shape[1:])) * 4 + 31) // 32 * 32
            assert cur[0] <= o_const, cur[0] - o_const
            return at(name, shape, dt, o)

        x_in = take("x_in", [P, XRING, TJ, DM])
        u = take("u", [P, L])
        w1 = take("w1", [P, L])
        lw = take("lw", [P, L])
        delta = take("delta", [P, L])
        dA = take("dA", [P, L])
        o_wr = cur[0]
        Bu = take("Bu", [P, L])
        hs = take("hs", [P, L])
        hT = take("hT", [P, KT, L + PAD])
        o_xc = cur[0]
        xc = take("xc", [P, 2, KT, L])
        diag = take("diag", [P, NB, KT, P])
        woutg = take("woutg", [P, NB, DM])
        o_bc = cur[0]
        assert o_bc + (NB - 1) * MODW * 4 >= o_acc + FIRST * SUB * DM * 4
        bc = take("bc", [P, NB, MODW])
        wx_sb = take("wx_sb", [P, KT, 2 * S + 1])
        wdb = take("wdb", [P, KT, P])
        win_sb = take("win_sb", [P, KT, S])
        wout_sb = take("wout_sb", [P, DM])
        junk = take("junk", [P, DM])
        slots = [o_bc, o_bc + KT * 2048, o_bc + 2 * KT * 2048, o_whi, o_whi + KT * 2048, o_wlo]
        wm = [at(f"wm{n}", [P, KT, 512], F32, o) for n, o in enumerate(slots)]
        wr = at("wr", [P, NE, DM], F32, o_wr)
        ga_bc = at("ga_bc", [P, NB, DM], F32, o_wlo + CHB + TJ * DM * 4)
        modrow = at("modrow", [NB, 4, DM], F32, o_raw)
        packed = at("packed", [NB, MODW], F32, o_raw + 4 * DM * 4)

        cur = [o_const]
        top = 229368 - base

        def const(name, shape, dt=F32):
            o = cur[0]
            cur[0] += (int(np.prod(shape[1:])) * 4 + 31) // 32 * 32
            assert cur[0] <= top, cur[0] - top
            return at(name, shape, dt, o)

        ident = const("ident", [P, P])
        before = const("before", [P, P])
        ones = const("ones", [P, P])
        wdiff = const("wdiff", [P, DM])
        gap = const("gap", [P, ROW])
        c_sb = const("c_sb", [P, KT * NB])
        sc = const("sc", [P, KT * NB])
        sct = const("sct", [P, KT * NB])
        cw = const("cw", [P, KT, TAPS])
        cb = const("cb", [P, KT])
        Dv = const("Dv", [P, KT])
        Al = const("Al", [P, 1])
        Acol = const("Acol", [P, 1])
        cols = const("cols", [P, 3, KT, NB])
        Dga = const("Dga", [P, KT, NB])
        st = const("st", [P, TJ, 6])
        mv = const("mv", [P, TJ, 2])
        ve = const("ve", [P, TJ])
        nmean = const("nmean", [P, TJ])
        sumsq = const("sumsq", [P, TJ])
        eps_col = const("eps_col", [P, 1])
        r0 = const("r0", [P, TJ])
        lnv = const("lnv", [P, TJ])
        tt = const("tt", [P, TJ])
        rs = const("rs", [P, TJ])
        nm = const("nm", [P, TJ])
        st2 = const("st2", [P, TJ, 6])
        mv2 = const("mv2", [P, TJ, 2])
        ve2 = const("ve2", [P, TJ])
        r02 = const("r02", [P, TJ])
        lnv2 = const("lnv2", [P, TJ])
        tt2 = const("tt2", [P, TJ])
        rs2 = const("rs2", [P, TJ])
        nm2 = const("nm2", [P, TJ])
        lg = const("lg", [P, TJ])
        m1 = const("m1", [P, TJ])
        al = const("al", [P, TJ])
        eal = const("eal", [P, TJ])
        den = const("den", [P, TJ])
        incl = const("incl", [P, TJ])
        rank = const("rank", [P, TJ])
        pos = const("pos", [P, TJ])
        run = const("run", [P, 1])
        posI = const("posI", [P, 2, TJ], I32)
        tokbat = const("tokbat", [P, NB * TJ, 2], I32)
        tokF = const("tokF", [P, NB * TJ])
        back = const("back", [P, NB * TJ])
        n0f = const("n0f", [P, 1])
        n0I = const("n0I", [P, 1], I32)
        firstf = const("firstf", [P, 1])
        firstI = const("firstI", [P, 1], I32)
        gapf = const("gapf", [P, SUB])
        gapI = const("gapI", [P, SUB], I32)

        bank = [psum(f"bank{i}") for i in range(8)]
        pT = bank[0:2]
        pB, pC, pD, pX = bank[2:6]
        pR = bank[6:8]
        hP = bank[0:2]
        yP = bank[2:4]
        xP = bank[4:6]

        ga_dram = nc.dram_tensor("ga_rows", [NB, DM], F32, kind="Internal").ap()
        gb_dram = nc.dram_tensor("gb_rows", [NB, DM], F32, kind="Internal").ap()
        mod_dram = nc.dram_tensor("mod_rows", [NB, MODW], F32, kind="Internal").ap()
        rows_dram = nc.dram_tensor("sorted_tokens", [ROWS, DM], F32, kind="Internal").ap()
        res_dram = nc.dram_tensor("sorted_residuals", [ROWS, ROW], F32, kind="Internal").ap()

        s_c = sem("c_landed")
        s_wm = [sem(f"wmod_landed{i}") for i in range(6)]
        s_small = sem("small_landed")
        s_wt = sem("mixer_weights_landed")
        s_wr = sem("router_landed")
        s_gbc = sem("ga_broadcast_landed")
        s_bc = [sem(f"mod_broadcast_landed{b}") for b in range(NB)]
        s_md = sem("mod_stored")
        s_x = [sem(f"x_landed{b}") for b in range(NB)]
        s_raw = [sem("raw_fc_landed"), sem("raw_proj_landed")]
        s_xs = [sem(f"sorted_landed{i}") for i in range(NT)]
        s_rr = [[sem(f"res_row_landed{o}_{i}") for i in range(SUB)] for o in range(RING)]
        s_sc1 = sem("tokens_scattered")
        s_sc2 = [sem(f"residuals_scattered{i}") for i in range(2)]
        SC2_TOTAL = (16 * (NB // 2 * TJ + SUB), 16 * NB // 2 * TJ)
        s_gr = [[sem(f"gb_row_landed{o}_{i}") for i in range(SUB)] for o in range(RING)]
        s_out = [[sem(f"out_scattered{o}_{i}") for i in range(SUB)] for o in range(RING)]
        s_pass = sem("waits_passed")
        s_const = sem("pool_consts")
        s_dconst = sem("dve_consts")
        s_sil = sem("silu_exp_done")
        s_silu = sem("silu_ready")
        s_mc = sem("mod_columns_done")
        s_cols = sem("mod_columns_ready")
        s_mm = sem("mod_row_done")
        s_mr = sem("mod_row_ready")
        s_g5 = sem("gb_row_copied")
        s_wdb = sem("delta_weights_ready")
        s_Dga = sem("D_ga_ready")
        s_diag = sem("diagonals_ready")
        s_wd = sem("router_difference_ready")
        s_wg = sem("out_weights_ready")
        s_A = sem("A_exp_done")
        s_An = sem("A_ready")
        s_zz = sem("mixer_stats_ready")
        s_nmean = sem("negative_mean_ready")
        s_sumsq = sem("square_sum_ready")
        s_l0 = sem("mixer_ln_step")
        s_r0 = sem("mixer_rstd_guess")
        s_rs = sem("mixer_rstd_ready")
        s_z = sem("z_ready")
        s_zT = sem("zT_done")
        s_hT = sem("hT_ready")
        s_y0 = sem("last_tap_ready")
        s_cv = sem("conv_done")
        s_pd = sem("delta_product_done")
        s_pb = sem("B_C_products_done")
        s_px = sem("state_product_done")
        s_ab = sem("abs_ready")
        s_u = sem("exp_minus_abs_ready")
        s_w1 = sem("one_plus_u_ready")
        s_lw = sem("log_ready")
        s_dl = sem("delta_ready")
        s_dA = sem("decay_ready")
        s_bu = sem("Bu_ready")
        s_hm = sem("state_ready")
        s_y = sem("mixer_output_done")
        s_x2 = sem("x2_ready")
        s_ve2 = sem("expert_stats_ready")
        s_l2 = sem("expert_ln_step")
        s_r2 = sem("expert_rstd_guess")
        s_rs2 = sem("expert_rstd_ready")
        s_z2 = sem("z2_ready")
        s_lg = sem("margin_products_ready")
        s_h2m = sem("h2_scaled")
        s_h2 = sem("h2_ready_pool")
        s_h2d = sem("h2_ready_dve")
        s_al = sem("margin_ready")
        s_ea = sem("margin_exp_ready")
        s_tw = sem("top_weight_ready")
        s_pad = sem("residual_padding_ready")
        s_m1 = sem("expert_mask_ready")
        s_pf = sem("prefix_counts_done")
        s_rk = sem("ranks_ready")
        s_pos = sem("positions_ready")
        s_tid = sem("token_numbers_ready")
        s_n0 = sem("count_ready")
        s_first = sem("early_count_ready")
        s_dve = sem("dve_steps")
        s_xt = sem("sorted_transposed")
        s_xhi = sem("sorted_hi_ready")
        s_xlo = sem("sorted_lo_ready")
        s_whi = sem("weights_hi_ready")
        s_wlo = sem("weights_lo_ready")
        s_h = [sem(f"h_done{m}") for m in range(HM)]
        s_relu = [sem(f"relu_ready{m}") for m in range(HM)]
        s_q = [sem(f"twice_h_ready{m}") for m in range(HM)]
        s_ah = [sem(f"a_hi_ready{m}") for m in range(HM)]
        s_af = [sem(f"a_full_ready{m}") for m in range(HM)]
        s_al2 = [sem(f"a_lo_ready{m}") for m in range(HM)]
        s_yy = [sem(f"y_done{s}") for s in range(SUB)]
        s_au = [sem("a_used0"), s_yy[SUB - 1]]
        s_yu = [sem(f"y_used{s}") for s in range(SUB)]
        s_fin = sem("final_steps")
        s_or = [sem(f"out_row_ready{s}") for s in range(SUB)]

        EARLY = {1: (0, 1, 2), 2: (3, 4, 5), 3: (6, 7)}
        IN_RAW = min(RING, CHB // (SUB * ROW * 4))
        DVE_H2 = (2, 3)

        def h2_by_pool(b):
            return [j for j in range(TJ) if not (b == NB - 1 and j in DVE_H2)]

        def z2_by_act(b):
            return [j for j in range(TJ) if not (b == NB - 1 and j in DVE_H2)]

        def next_rows(t):
            return (t + 1,) if t == FIRST else (t + 1,) if FIRST < t < NT - 1 else ()

        def split_after(t):
            return range(FIRST) if t == FIRST else (t - 1,) if t > FIRST else ()

        def out_bank(b, j):
            return (pD, pT[0], pT[1], pX)[j] if b == NB - 1 else (pD, pR[1], pR[0], pX)[j]

        block = ctx.enter_context(nc.Block())

        @block.sync
        def _(sp):
            def load_wmod(n, row):
                sp.dma_start(wm[n][:, :, :], wmod[row]).then_inc(s_wm[n], 16)

            def load_x(b):
                wait(sp, s_x2, TJ * (b - XRING + 1))
                sp.dma_start(x_in[:, b % XRING], x[b]).then_inc(s_x[b], 16)

            def load_rows(tiles):
                for t in tiles:
                    sp.dma_start(sorted_rows[:, SUB * t:SUB * t + SUB],
                                 rows_dram[TILE * t:TILE * t + TILE].rearrange("(s p) d -> p s d", p=P)).then_inc(s_xs[t], 16)

            sp.dma_start(c_sb[:, :], cT).then_inc(s_c, 16)
            load_wmod(0, 1)
            load_x(0)
            load_wmod(1, 0)
            for dst, src in ((cw[:, :, :], conv_w), (cb[:, :], conv_b), (Dv[:, :], Dvec), (Al[:, :], A_log)):
                sp.dma_start(dst, src).then_inc(s_small, 16)
            load_wmod(2, 2)
            for dst, src in ((wx_sb[:, :, :], wx), (win_sb[:, :, :], win), (wout_sb[:, :], wout)):
                sp.dma_start(dst, src).then_inc(s_wt, 16)
            load_x(1)
            load_wmod(3, 4)
            sp.dma_start(wr[:, :, :].rearrange("p e d -> p (e d)"),
                         w_router.rearrange("e d -> (e d)").partition_broadcast(P)).then_inc(s_wr, 16)
            load_x(2)
            load_wmod(4, 3)
            load_wmod(5, 5)
            sp.wait_ge(s_mr, 3)
            sp.dma_start(ga_dram, modrow[:, 2, :]).then_inc(s_md, 16)
            sp.wait_ge(s_md, 16)
            for b in range(NB):
                sp.dma_start(ga_bc[:, b, :], ga_dram[b].partition_broadcast(P)).then_inc(s_gbc, 16)
            load_x(3)
            sp.wait_ge(s_mr, 5)
            sp.dma_start(mod_dram, packed[:, :]).then_inc(s_md, 16)
            sp.wait_ge(s_md, 32)
            for b in range(NB):
                sp.dma_start(bc[:, b, :], mod_dram[b].partition_broadcast(P)).then_inc(s_bc[b], 16)
            sp.wait_ge(s_mr, 6)
            sp.dma_start(gb_dram, modrow[:, 3, :]).then_inc(s_md, 16)
            sp.wait_ge(s_md, 48)
            for i in range(2):
                sp.dma_start(raw[:, 4 * i:4 * i + 4], wffn[0][:, 4 * i:4 * i + 4]).then_inc(s_raw[i], 16)
            sp.wait_ge(s_x2, TJ * NB)
            sp.wait_ge(s_first, 1)
            early_rows = sp.value_load(firstI[0:1, 0:1], min_val=0, max_val=(NB - 1) * L)
            with sp.If(early_rows > FIRST * TILE - 1):
                sp.wait_ge(s_sc1, 16 * (NB - 1) * TJ)
            with sp.Else():
                sp.wait_ge(s_sc1, 16 * (NB * TJ + SUB))
            load_rows(range(FIRST))
            def second_block(i):
                sp.wait_ge(s_whi, 4 * i + 4)
                sp.wait_ge(s_wlo, 4 * i + 4)
                sp.dma_start(raw[:, 4 * i:4 * i + 4], wffn[1, :, 4 * i:4 * i + 4]).then_inc(s_raw[i], 16)

            second_block(0)
            sp.wait_ge(s_sc1, 16 * (NB * TJ + SUB))
            load_rows(range(FIRST, NT))
            second_block(1)
            with sp.Fori(2, NHB) as hb:
                for i in range(2):
                    sp.wait_ge(s_whi, CH * (hb - 1) + 4 * i + 4)
                    sp.wait_ge(s_wlo, CH * (hb - 1) + 4 * i + 4)
                    sp.dma_start(raw[:, 4 * i:4 * i + 4], wffn[hb, :, 4 * i:4 * i + 4]).then_inc(s_raw[i], 16)
            sp.wait_ge(s_whi, CH * NHB)
            sp.wait_ge(s_wlo, CH * NHB)
            for i in range(2):
                sp.wait_ge(s_sc2[i], SC2_TOTAL[i])

            def load_residuals(tiles):
                for t in tiles:
                    for s in range(SUB):
                        wait(sp, s_out[t % RING][s], 16 * (t // RING))
                        sp.dma_start(res_row[t % RING][s][:, :], res_dram[TILE * t + P * s:TILE * t + P * s + P, :]).then_inc(s_rr[t % RING][s], 16)

            load_residuals(range(IN_RAW))
            sp.wait_ge(s_yy[SUB - 1], NT * (NHB - 1))
            load_residuals(range(IN_RAW, NT))

        @block.gpsimd
        def _(pool):
            pool.memset(ident[:, :], 0.0).then_inc(s_const, 1)
            pool.memset(before[:, :], 1.0).then_inc(s_const, 1)
            pool.iota(tokbat[:, :, 0], pattern=[[P, NB * TJ]], base=0, channel_multiplier=1).then_inc(s_const, 1)
            pool.iota(tokbat[:, :, 1], pattern=[[1, NB], [0, TJ]], base=0, channel_multiplier=0).then_inc(s_const, 1)
            pool.memset(gap[:, :], 0.0).then_inc(s_const, 1)
            pool.wait_ge(s_const, 5)
            pool.affine_select(out=ident[:, :], in_=ident[:, :], compare_op=ALU.not_equal, fill=1.0, base=0,
                               pattern=[[-1, P]], channel_multiplier=1).then_inc(s_const, 1)
            pool.affine_select(out=before[:, :], in_=before[:, :], compare_op=ALU.is_gt, fill=0.0, base=0,
                               pattern=[[1, P]], channel_multiplier=-1).then_inc(s_const, 1)
            pool.iota(gap[:, DM + 1:DM + 2].bitcast(I32), pattern=[[0, 1]], base=NO_TOKEN,
                      channel_multiplier=0).then_inc(s_const, 1)
            pool.wait_ge(s_const, 8)

            pool.wait_ge(s_wt, 48)
            pool.wait_ge(s_gbc, 16 * NB)
            for b in range(NB):
                pool.tensor_tensor(woutg[:, b, :], wout_sb[:, :], ga_bc[:, b, :], ALU.mult).then_inc(s_wg, 1)
            pool.memset(res[:, :, :, DM:ROW], 0.0).then_inc(s_pad, 1)
            pool.wait_ge(s_pad, 1)

            def low(hb, c):
                pool.wait_ge(s_whi, CH * hb + c + 1)
                pool.tensor_tensor(Wlo[:, hb % 2, c, :], raw[:, c, :], Whi[:, hb % 2, c, :].bitcast(F32),
                                   ALU.subtract).then_inc(s_wlo, 1)

            for b in range(NB):
                wait(pool, s_sc2[b % 2], 16 * TJ * (b // 2))
                pool.tensor_copy(res[:, b % 2, :, DM + 1:DM + 3].bitcast(I32), tokbat[:, TJ * b:TJ * b + TJ, :]).then_inc(s_tid, 1)
                if b < NB - 1:
                    for c in EARLY.get(b, ()):
                        low(0, c)
                pool.wait_ge(s_bc[b], 16)
                for n, j in enumerate(h2_by_pool(b)):
                    pool.wait_ge(s_lg, TJ * b + j + 1)
                    pool.tensor_tensor(h2[:, j, :], h2[:, j, :], bc[:, b, 0:DM], ALU.mult).then_inc(s_h2m, 1)
                    pool.wait_ge(s_h2m, TJ * b + n + 1)
                    pool.tensor_tensor(h2[:, j, :], h2[:, j, :], bc[:, b, DM:2 * DM], ALU.add).then_inc(s_h2, 1)
                pool.wait_ge(s_pos, b + 1)
                pool.wait_ge(s_h2, TJ * b + len(h2_by_pool(b)))
                for j in range(TJ):
                    if b == NB - 1 and j in DVE_H2:
                        pool.wait_ge(s_h2d, DVE_H2.index(j) + 1)
                    pool.indirect_dma_start(out=rows_dram, out_offset=bass.IndirectOffsetOnAxis(ap=posI[:, b % 2, j:j + 1], axis=0),
                                            in_=h2[:, j, :], in_offset=None).then_inc(s_sc1, 16)
                if b == NB - 1:
                    pool.wait_ge(s_n0, 2)
                    for g in range(SUB):
                        pool.indirect_dma_start(out=rows_dram, out_offset=bass.IndirectOffsetOnAxis(ap=gapI[:, g:g + 1], axis=0),
                                                in_=gap[:, 0:DM], in_offset=None).then_inc(s_sc1, 16)
                    for c in EARLY[b]:
                        low(0, c)
                pool.wait_ge(s_tw, b + 1)
                pool.wait_ge(s_tid, b + 1)
                for j in range(TJ):
                    pool.indirect_dma_start(out=res_dram, out_offset=bass.IndirectOffsetOnAxis(ap=posI[:, b % 2, j:j + 1], axis=0),
                                            in_=res[:, b % 2, j, :], in_offset=None).then_inc(s_sc2[b % 2], 16)
            for g in range(SUB):
                pool.indirect_dma_start(out=res_dram, out_offset=bass.IndirectOffsetOnAxis(ap=gapI[:, g:g + 1], axis=0),
                                        in_=gap[:, :], in_offset=None).then_inc(s_sc2[0], 16)

            pool.wait_ge(s_sc1, 16 * (NB * TJ + SUB))
            with pool.Fori(1, NHB) as hb:
                with pool.Fori(0, CH) as c:
                    low(hb, c)
            def gather_gb(t):
                for s in range(SUB):
                    pool.wait_ge(s_rr[t % RING][s], 16 * (t // RING + 1))
                    wait(pool, s_or[s], t - RING + 1)
                    pool.indirect_dma_start(out=gb_row[t % RING][s][:, :], out_offset=None, in_=gb_dram,
                                            in_offset=bass.IndirectOffsetOnAxis(
                                                ap=res_row[t % RING][s][:, DM + 2:DM + 3].bitcast(I32), axis=0)).then_inc(s_gr[t % RING][s], 16)

            pool.wait_ge(s_yy[SUB - 1], NT * (NHB - 1))
            for t in range(RING - 1):
                gather_gb(t)
            for t in range(NT):
                for s in range(SUB):
                    pool.wait_ge(s_or[s], t + 1)
                    pool.indirect_dma_start(out=out, out_offset=bass.IndirectOffsetOnAxis(
                                                ap=res_row[t % RING][s][:, DM + 1:DM + 2].bitcast(I32), axis=0),
                                            in_=acc[:, SUB * t + s, :], in_offset=None, bounds_check=TOK - 1,
                                            oob_is_err=False).then_inc(s_out[t % RING][s], 16)
                if t + RING - 1 < NT:
                    gather_gb(t + RING - 1)
            for t in range(NT - RING, NT):
                for s in range(SUB):
                    pool.wait_ge(s_out[t % RING][s], 16 * (t // RING + 1))

        @block.scalar
        def _(act):
            def stats1(b):
                act.wait_ge(s_x[b], 16)
                wait(act, s_rs, b)
                act.wait_ge(s_zT, KT * b)
                for j in range(TJ):
                    act.activation(z[:, j, :], x_in[:, b % XRING, j, :], ACT.Identity, scale=-1.0 / DM,
                                   accum_out=nmean[:, j:j + 1]).then_inc(s_nmean, 1)
                for j in range(TJ):
                    act.wait_ge(s_nmean, TJ * (b - 1) + j + 1)
                    act.activation(z[:, j, :], x_in[:, b % XRING, j, :], ACT.Square, bias=nmean[:, j:j + 1],
                                   accum_out=sumsq[:, j:j + 1]).then_inc(s_sumsq, 1)

            def guess1(b):
                if b == 0:
                    act.wait_ge(s_zz, 1)
                    act.activation(lnv[:, :], ve[:, :], ACT.Ln).then_inc(s_l0, 1)
                else:
                    act.wait_ge(s_sumsq, TJ * b)
                    act.activation(lnv[:, :], sumsq[:, :], ACT.Ln, bias=eps_col[:, 0:1], scale=1.0 / DM).then_inc(s_l0, 1)
                act.wait_ge(s_l0, b + 1)
                act.activation(r0[:, :], lnv[:, :], ACT.Exp, scale=-0.5).then_inc(s_r0, 1)

            def normalize1(b):
                act.wait_ge(s_rs, b + 1)
                wait(act, s_zT, KT * b)
                for j in range(TJ):
                    act.activation(z[:, j, :], x_in[:, b % XRING, j, :], ACT.Identity, bias=nm[:, j:j + 1],
                                   scale=rs[:, j:j + 1]).then_inc(s_z, 1)

            def modulate1(b):
                wait(act, s_cv, KT * b)
                wait(act, s_pb, 2 * b)
                for k in range(KT):
                    act.wait_ge(s_zT, KT * b + k + 1)
                    act.activation(hT[:, k, PAD:PAD + L], pT[k % 2][:, :], ACT.Identity,
                                   bias=cols[:, 0, k, b:b + 1], scale=cols[:, 1, k, b:b + 1]).then_inc(s_hT, 1)
                if b >= 2:
                    margin_exp(b - 2)
                wait(act, s_y, TJ * (b - 1))
                for k in range(KT):
                    act.wait_ge(s_hT, KT * b + k + 1)
                    act.activation(xc[:, b % 2, k, :], hT[:, k, PAD:PAD + L], ACT.Identity,
                                   bias=cb[:, k:k + 1], scale=cw[:, k, PAD:TAPS]).then_inc(s_y0, 1)

            def exp_minus_abs(b):
                act.wait_ge(s_pd, b + 1)
                wait(act, s_dl, b)
                act.activation(u[:, :], pD[:, :], ACT.Abs).then_inc(s_ab, 1)
                act.wait_ge(s_ab, b + 1)
                act.activation(u[:, :], u[:, :], ACT.Exp, scale=-1.0).then_inc(s_u, 1)

            def log_part(b):
                act.wait_ge(s_w1, b + 1)
                act.activation(lw[:, :], w1[:, :], ACT.Ln).then_inc(s_lw, 1)

            def decay(b):
                act.wait_ge(s_dl, b + 1)
                wait(act, s_hm, b)
                act.activation(dA[:, :], delta[:, :], ACT.Exp, scale=Acol[:, 0:1]).then_inc(s_dA, 1)

            def guess2(b):
                act.wait_ge(s_ve2, b + 1)
                act.activation(lnv2[:, :], ve2[:, :], ACT.Ln).then_inc(s_l2, 1)
                act.wait_ge(s_l2, b + 1)
                act.activation(r02[:, :], lnv2[:, :], ACT.Exp, scale=-0.5).then_inc(s_r2, 1)

            def normalize2(b):
                act.wait_ge(s_rs2, b + 1)
                wait(act, s_sc1, 16 * TJ * b)
                for j in z2_by_act(b):
                    act.activation(h2[:, j, :], res[:, b % 2, j, 0:DM], ACT.Identity, bias=nm2[:, j:j + 1],
                                   scale=rs2[:, j:j + 1]).then_inc(s_z2, 1)

            def margin_exp(b):
                act.wait_ge(s_al, b + 1)
                act.activation(eal[:, :], al[:, :], ACT.Exp, scale=-1.0).then_inc(s_ea, 1)

            def diagonals(b):
                for k in range(KT):
                    act.activation(diag[:, b, k, :], ident[:, :], ACT.Identity, scale=Dga[:, k, b:b + 1]).then_inc(s_diag, 1)

            def split(hb, c):
                act.activation(Whi[:, hb % 2, c, :], raw[:, c, :], ACT.Copy).then_inc(s_whi, 1)

            act.preload_act_table_set("natural_log_exp_and_others")
            act.wait_ge(s_c, 16)
            act.activation(sc[:, :], c_sb[:, :], ACT.Exp, scale=-1.0).then_inc(s_sil, 1)
            guess1(0)
            act.wait_ge(s_small, 64)
            act.activation(Acol[:, :], Al[:, :], ACT.Exp).then_inc(s_A, 1)
            normalize1(0)
            act.wait_ge(s_cols, 1)
            act.wait_ge(s_dconst, 3)
            modulate1(0)
            exp_minus_abs(0)
            log_part(0)
            stats1(1)
            guess1(1)
            act.wait_ge(s_An, 1)
            decay(0)
            act.wait_ge(s_const, 8)
            act.wait_ge(s_Dga, KT)
            diagonals(0)
            normalize1(1)
            modulate1(1)
            for b in range(NB):
                if b + 2 < NB:
                    stats1(b + 2)
                    guess1(b + 2)
                if b + 1 < NB:
                    diagonals(b + 1)
                for c in EARLY.get(b, ()):
                    act.wait_ge(s_raw[c // 4], 16)
                    split(0, c)
                if b + 1 < NB:
                    exp_minus_abs(b + 1)
                    log_part(b + 1)
                if b + 2 < NB:
                    normalize1(b + 2)
                if b + 1 < NB:
                    decay(b + 1)
                guess2(b)
                if b == 0:
                    act.wait_ge(s_wg, NB)
                normalize2(b)
                if b + 2 < NB:
                    modulate1(b + 2)
                else:
                    margin_exp(b)

            def high_rows(t):
                for s in range(SUB * t, SUB * t + SUB):
                    act.wait_ge(s_xt, s + 1)
                    act.activation(XShi[:, :, P * s:P * s + P], xP[s % 2][:, :].rearrange("p (k t) -> p k t", k=KT),
                                   ACT.Copy).then_inc(s_xhi, 1)

            def job(hb, t, between=()):
                i = NT * hb + t
                for m in range(HM):
                    act.wait_ge(s_h[m], i + 1)
                    wait(act, s_q[m], i)
                    act.activation(relu_h[:, m, :], hP[m][:, 0:TILE], ACT.Relu).then_inc(s_relu[m], 1)
                for n in between:
                    high_rows(n)
                for m in range(HM):
                    act.wait_ge(s_q[m], i + 1)
                    wait(act, s_au[m], i)
                    act.activation(ahi[:, m, :], twice_h[:, m, :], ACT.Square, scale=0.5).then_inc(s_ah[m], 1)
                    wait(act, s_al2[m], i)
                    act.activation(a_full[:, m, :], twice_h[:, m, :], ACT.Square, scale=0.5).then_inc(s_af[m], 1)

            for t in range(FIRST):
                high_rows(t)
            for t in range(NT):
                for n in next_rows(t):
                    high_rows(n)
                job(0, t, (FIRST,) if t == FIRST - 1 else ())
                if t == FIRST:
                    for i in range(2):
                        act.wait_ge(s_sc2[i], SC2_TOTAL[i])
                for c in split_after(t):
                    act.wait_ge(s_raw[c // 4], 32)
                    split(1, c)
            with act.Fori(1, NHB - 1) as hb:
                job(hb, 0)
                act.wait_ge(s_yy[SUB - 1], NT * hb)
                for i in range(2):
                    with act.Fori(4 * i, 4 * i + 4) as c:
                        job(hb, c + 1)
                        act.wait_ge(s_raw[i], 16 * (hb + 2))
                        split(hb + 1, c)
            with act.Fori(0, NT) as t:
                job(NHB - 1, t)

        @block.tensor
        def _(pe):
            def mod_row(r):
                wait(pe, s_mr, r - 1)
                if r >= 4:
                    pe.wait_ge(s_x2, r - 1)
                pe.wait_ge(s_wm[r], 16)
                for k in range(KT):
                    mm = pe.matmul(pR[r % 2][0:NB, :], sc[:, NB * k:NB * k + NB], wm[r][:, k, :],
                                   start=(k == 0), stop=(k == KT - 1))
                mm.then_inc(s_mm, 1)

            def mod_columns(rows):
                for n in rows:
                    for k in range(KT):
                        o = NB * (KT * n + k)
                        mm = pe.transpose(pX[:, o:o + NB], modrow[0:NB, n, P * k:P * k + P], ident[0:NB, 0:NB])
                mm.then_inc(s_mc, 1)

            def transposes1(b, ks=range(KT)):
                for k in ks:
                    wait(pe, s_hT, KT * b + k - 1)
                    for j in range(TJ):
                        if k == 0:
                            pe.wait_ge(s_z, TJ * b + j + 1)
                        mm = pe.transpose(pT[k % 2][:, P * j:P * j + P], z[:, j, P * k:P * k + P], ident[:, :])
                    mm.then_inc(s_zT, 1)

            def delta_product(b):
                wait(pe, s_dl, b)
                for k in range(KT):
                    pe.wait_ge(s_hT, KT * b + k + 1)
                    mm = pe.matmul(pD[:, :], wdb[:, k, :], hT[:, k, PAD:PAD + L], start=(k == 0), stop=(k == KT - 1))
                mm.then_inc(s_pd, 1)

            def B_C_products(b):
                wait(pe, s_hm, b)
                for n, bk in enumerate((pB, pC)):
                    for k in range(KT):
                        mm = pe.matmul(bk[:, :], wx_sb[:, k, S * n:S * n + S], hT[:, k, PAD:PAD + L],
                                       start=(k == 0), stop=(k == KT - 1))
                    mm.then_inc(s_pb, 1)

            def state_product(b):
                for k in range(KT):
                    pe.wait_ge(s_cv, KT * b + k + 1)
                    mm = pe.matmul(pX[:, :], win_sb[:, k, :], xc[:, b % 2, k, :], start=(k == 0), stop=(k == KT - 1))
                mm.then_inc(s_px, 1)

            def skip_product(b, j):
                wait(pe, s_x2, TJ * b)
                out_j = out_bank(b, j)
                if out_j is pD:
                    pe.wait_ge(s_dl, b + 1)
                elif out_j in pT:
                    pe.wait_ge(s_hT, KT * NB)
                elif out_j is pX:
                    pe.wait_ge(s_bu, b + 1)
                else:
                    if out_j is pR[0]:
                        wait(pe, s_rk, b)
                    else:
                        wait(pe, s_x2, TJ * b)
                    if b == 0:
                        pe.wait_ge(s_mr, 4)
                    else:
                        pe.wait_ge(s_g5, 1)
                pe.wait_ge(s_diag, KT * (b + 1))
                for m in range(KT):
                    pe.matmul(out_j[:, P * m:P * m + P], xc[:, b % 2, m, P * j:P * j + P], diag[:, b, m, :],
                              start=(m == 0), stop=False)

            def state_output(b, j):
                pe.matmul(out_bank(b, j)[:, :], hs[:, P * j:P * j + P], woutg[:, b, :], start=False, stop=True).then_inc(s_y, 1)

            def early_skips(b):
                return (0, 1, 2) if b == NB - 1 else (0, 1) if b > 0 else (0,)

            def mixer_output(b):
                for j in (3, 1, 2):
                    if j not in early_skips(b):
                        skip_product(b, j)
                pe.wait_ge(s_hm, b + 1)
                pe.wait_ge(s_wg, b + 1)
                for j in range(TJ):
                    state_output(b, j)

            def prefix(b):
                if b == 0:
                    pe.wait_ge(s_g5, 1)
                pe.wait_ge(s_m1, b + 1)
                pe.wait_ge(s_x2, TJ * (b + 1))
                pe.matmul(pR[0][:, 0:TJ], before[:, :], m1[:, :], start=True, stop=True).then_inc(s_pf, 1)
                pe.matmul(pR[0][:, TJ:2 * TJ], ones[:, :], m1[:, :], start=True, stop=True).then_inc(s_pf, 1)

            pe.wait_ge(s_silu, 1)
            mod_row(0)
            mod_row(1)
            pe.wait_ge(s_const, 8)
            pe.wait_ge(s_mr, 2)
            mod_columns((0, 1))
            mod_row(2)
            transposes1(0)
            pe.wait_ge(s_wdb, 1)
            delta_product(0)
            B_C_products(0)
            pe.wait_ge(s_mr, 3)
            pe.wait_ge(s_cols, 1)
            mod_columns((2,))
            mod_row(3)
            pe.wait_ge(s_cols, 2)
            state_product(0)
            transposes1(1)
            skip_product(0, 0)
            for b in range(NB):
                mixer_output(b)
                if b + 1 < NB:
                    pe.wait_ge(s_x2, TJ * b + 1)
                    delta_product(b + 1)
                if b == 0:
                    mod_row(4)
                    mod_row(5)
                if b + 1 < NB:
                    B_C_products(b + 1)
                    state_product(b + 1)
                if b + 2 < NB:
                    transposes1(b + 2, (0, 1))
                if b + 1 < NB:
                    for j in early_skips(b + 1):
                        skip_product(b + 1, j)
                prefix(b)
                if b + 2 < NB:
                    transposes1(b + 2, (2, 3))

            def transpose_rows(t):
                for s in range(SUB * t, SUB * t + SUB):
                    pe.wait_ge(s_xs[t], 16)
                    wait(pe, s_xhi, s - 1)
                    wait(pe, s_xlo, s - 1)
                    for k in range(KT):
                        mm = pe.transpose(xP[s % 2][:, P * k:P * k + P], sorted_rows[:, s, P * k:P * k + P], ident[:, :])
                    mm.then_inc(s_xt, 1)

            PARTS = ((0, 0), (0, 1), (1, 0))
            W, XS, A = (Whi, Wlo), (XShi, XSlo), (ahi, alo)

            def fc(par, hb, t):
                i = NT * hb + t

                def body(e):
                    for m in range(HM):
                        n = 0
                        for k in range(KT):
                            for wp, xp in PARTS:
                                o = HB * (k % 2) + P * m
                                mm = pe.matmul(hP[m][:, 0:TILE], W[wp][:, par, 2 * e + k // 2, o:o + P],
                                               XS[xp][:, k, bass.ds(t * TILE, TILE)],
                                               start=(n == 0), stop=(n == 3 * KT - 1))
                                n += 1
                        mm.then_inc(s_h[m], 1)

                for m in range(HM):
                    wait(pe, s_q[m], i)
                with pe.If(n0 > t * TILE):
                    body(0)
                with pe.Else():
                    body(1)

            def proj(par, hb, t):
                i = NT * hb + t

                def body(e, subs):
                    for m in range(HM):
                        for s in range(SUB):
                            if s not in subs:
                                if m == HM - 1:
                                    pe.matmul(yP[s][:, :], ahi[:, m, P * s:P * s + P], Whi[:, par, 4 + 2 * e + m, :],
                                              start=True, stop=True).then_inc(s_yy[s], 1)
                                continue
                            for n, (ap, wp) in enumerate(PARTS):
                                mm = pe.matmul(yP[s][:, :], A[ap][:, m, P * s:P * s + P], W[wp][:, par, 4 + 2 * e + m, :],
                                               start=(m == 0 and n == 0), stop=(m == HM - 1 and n == 2))
                            if m == HM - 1:
                                mm.then_inc(s_yy[s], 1)
                        if m < HM - 1:
                            mm.then_inc(s_au[m], 1)
                for m in range(HM):
                    pe.wait_ge(s_al2[m], i + 1)
                for s in range(SUB):
                    wait(pe, s_yu[s], i)
                with pe.If(n0 > t * TILE):
                    with pe.If(n0 > t * TILE + P):
                        body(0, (0, 1))
                    with pe.Else():
                        body(0, (0,))
                with pe.Else():
                    with pe.If(n0 > t * TILE - P):
                        body(1, (1,))
                    with pe.Else():
                        body(1, (0, 1))

            def fc_weights_ready(hb):
                pe.wait_ge(s_whi, CH * hb + CH // 2)
                pe.wait_ge(s_wlo, CH * hb + CH // 2)

            def proj_weights_ready(hb):
                pe.wait_ge(s_whi, CH * (hb + 1))
                pe.wait_ge(s_wlo, CH * (hb + 1))

            def rest_of_block(par, hb, last=False):
                fc(par, hb, 1)
                proj_weights_ready(hb)
                proj(par, hb, 0)
                with pe.Fori(2, NT) as t:
                    fc(par, hb, t)
                    proj(par, hb, t - 1)
                if not last:
                    fc_weights_ready(hb + 1)
                    fc(1 - par, hb + 1, 0)
                proj(par, hb, NT - 1)

            pe.wait_ge(s_rk, NB)
            for t in range(FIRST):
                transpose_rows(t)
            pe.wait_ge(s_n0, 2)
            n0 = pe.value_load(n0I[0:1, 0:1], min_val=0, max_val=TOK)
            fc_weights_ready(0)
            for t in range(NT):
                for n in next_rows(t):
                    transpose_rows(n)
                if t == FIRST:
                    proj(0, 0, t - 1)
                pe.wait_ge(s_xhi, SUB * (t + 1))
                pe.wait_ge(s_xlo, SUB * (t + 1))
                fc(0, 0, t)
                if t == FIRST - 1:
                    transpose_rows(FIRST)
                    proj_weights_ready(0)
                if t > 0 and t != FIRST:
                    proj(0, 0, t - 1)
            fc_weights_ready(1)
            fc(1, 1, 0)
            proj(0, 0, NT - 1)
            with pe.Fori(0, NHB // 2 - 1) as pair:
                rest_of_block(1, 2 * pair + 1)
                rest_of_block(0, 2 * pair + 2)
            rest_of_block(1, NHB - 1, last=True)

        @block.vector
        def _(dve):
            own = Steps(dve, s_dve)
            z2_done = {}

            def stats(rows, stt, mvt, vet, done):
                if rows is not None:
                    for j in range(TJ):
                        own.mark(dve.bn_stats(stt[:, j, :], rows(j)))
                own.settle()
                dve.sem_inc(s_pass, 1)
                for j in range(TJ):
                    own.mark(dve.bn_aggr(mvt[:, j, :], stt[:, j, :]))
                own.settle()
                dve.tensor_scalar(vet[:, :], mvt[:, :, 1], EPS, None, ALU.add).then_inc(done, 1)

            def newton1_steps(b):
                def first():
                    dve.wait_ge(s_r0, b + 1)
                    wait(dve, s_z, TJ * b)
                    own.mark(dve.tensor_tensor(tt[:, :], r0[:, :], r0[:, :], ALU.mult))
                    dve.wait_ge(s_sumsq, TJ * b)
                    own.link(dve.tensor_scalar(ve[:, :], sumsq[:, :], 1.0 / DM, EPS, ALU.mult, ALU.add))

                def second():
                    own.mark(dve.tensor_tensor(tt[:, :], tt[:, :], ve[:, :], ALU.mult))

                def third():
                    own.settle()
                    own.mark(dve.tensor_scalar(tt[:, :], tt[:, :], -0.5, 1.5, ALU.mult, ALU.add))

                def fourth():
                    own.settle()
                    own.link(dve.tensor_tensor(rs[:, :], r0[:, :], tt[:, :], ALU.mult))
                    dve.tensor_tensor(nm[:, :], nmean[:, :], rs[:, :], ALU.mult).then_inc(s_rs, 1)

                return first, second, third, fourth

            def newton(vet, guess, tmp, rst, mvt, nmt, ready):
                own.link(dve.tensor_tensor(tmp[:, :], guess[:, :], guess[:, :], ALU.mult))
                own.link(dve.tensor_tensor(tmp[:, :], tmp[:, :], vet[:, :], ALU.mult))
                own.link(dve.tensor_scalar(tmp[:, :], tmp[:, :], -0.5, 1.5, ALU.mult, ALU.add))
                own.link(dve.tensor_tensor(rst[:, :], guess[:, :], tmp[:, :], ALU.mult))
                dve.scalar_tensor_tensor(nmt[:, :], mvt[:, :, 0], -1.0, rst[:, :], ALU.mult, ALU.mult).then_inc(ready, 1)

            def stats1(b):
                dve.wait_ge(s_x[b], 16)
                wait(dve, s_rs, b)
                stats(lambda j: x_in[:, b % XRING, j, :], st, mv, ve, s_zz)

            def newton1(b):
                dve.wait_ge(s_r0, b + 1)
                dve.wait_ge(s_zz, b + 1)
                wait(dve, s_z, TJ * b)
                newton(ve, r0, tt, rs, mv, nm, s_rs)

            def conv(b, tap, ks, done):
                for k in ks:
                    if tap == 0:
                        dve.wait_ge(s_y0, KT * b + k + 1)
                    else:
                        dve.wait_ge(s_dve, done[k])
                    ins = dve.scalar_tensor_tensor(xc[:, b % 2, k, :], hT[:, k, tap:tap + L],
                                                   cw[:, k, tap:tap + 1], xc[:, b % 2, k, :], ALU.mult, ALU.add)
                    if tap < PAD - 1:
                        done[k] = own.mark(ins)
                    else:
                        ins.then_inc(s_cv, 1)

            def softplus_residue(b):
                dve.wait_ge(s_u, b + 1)
                wait(dve, s_lw, b)
                dve.tensor_scalar(w1[:, :], u[:, :], 1.0, None, ALU.add).then_inc(s_w1, 1)
                dve.wait_ge(s_w1, b + 1)
                own.link(dve.scalar_tensor_tensor(u[:, :], w1[:, :], -1.0, u[:, :], ALU.add, ALU.subtract))

            def softplus(b):
                dve.wait_ge(s_lw, b + 1)
                own.link(dve.tensor_tensor(lw[:, :], lw[:, :], u[:, :], ALU.subtract))
                wait(dve, s_dA, b)
                dve.scalar_tensor_tensor(delta[:, :], pD[:, :], 0.0, lw[:, :], ALU.max, ALU.add).then_inc(s_dl, 1)

            def scan(b):
                p = b - 1
                dve.wait_ge(s_dl, b + 1)
                dve.wait_ge(s_pb, 2 * b + 1)
                own.mark(dve.tensor_tensor(Bu[:, :], delta[:, :], pB[:, :], ALU.mult))
                if p >= 0:
                    row_candidates(p)
                own.settle()
                dve.wait_ge(s_px, b + 1)
                dve.tensor_tensor(Bu[:, :], Bu[:, :], pX[:, :], ALU.mult).then_inc(s_bu, 1)
                if p >= 0:
                    counts(p)
                dve.wait_ge(s_bu, b + 1)
                dve.wait_ge(s_dA, b + 1)
                wait(dve, s_y, TJ * b)
                own.mark(dve.tensor_tensor_scan(hs[:, :], dA[:, :], Bu[:, :], 0.0, ALU.mult, ALU.add))
                if p >= 0:
                    ranks(p)
                own.settle()
                dve.wait_ge(s_pb, 2 * b + 2)
                dve.tensor_tensor(hs[:, :], hs[:, :], pC[:, :], ALU.mult).then_inc(s_hm, 1)
                if p >= 0:
                    positions(p)
                    top_weight(p)

            def residual(b, j):
                dve.wait_ge(s_y, TJ * b + j + 1)
                dve.tensor_tensor(res[:, b % 2, j, 0:DM], out_bank(b, j)[:, :], x_in[:, b % XRING, j, :], ALU.add).then_inc(s_x2, 1)

            def stats2(b):
                dve.wait_ge(s_x2, TJ * (b + 1))
                wait(dve, s_rs2, b)
                rows = lambda j: res[:, b % 2, j, 0:DM]
                if b == NB - 1:
                    own.mark(dve.bn_stats(st2[:, TJ - 1, :], rows(TJ - 1)))
                    rows = None
                stats(rows, st2, mv2, ve2, s_ve2)

            def newton2(b):
                dve.wait_ge(s_r2, b + 1)
                dve.wait_ge(s_ve2, b + 1)
                wait(dve, s_z2, TJ * b)
                newton(ve2, r02, tt2, rs2, mv2, nm2, s_rs2)

            def margins(b):
                dve.wait_ge(s_bc[b], 16)
                for j in range(TJ):
                    if j in z2_by_act(b):
                        dve.wait_ge(s_z2, TJ * b + j + 1)
                    else:
                        dve.wait_ge(s_dve, z2_done[j])
                    dve.tensor_tensor_reduce(junk[:, :], h2[:, j, :], bc[:, b, 2 * DM:3 * DM], 1.0, 0.0, ALU.mult, ALU.add,
                                             lg[:, j:j + 1]).then_inc(s_lg, 1)
                    dve.wait_ge(s_lg, TJ * b + j + 1)
                own.link(dve.tensor_scalar(lg[:, :], lg[:, :], bc[:, b, 3 * DM:3 * DM + 1], None, ALU.add))
                dve.tensor_scalar(m1[:, :], lg[:, :], 0.0, None, ALU.is_gt).then_inc(s_m1, 1)
                dve.scalar_tensor_tensor(al[:, :], lg[:, :], -1.0, lg[:, :], ALU.mult, ALU.max).then_inc(s_al, 1)

            def row_candidates(b):
                dve.wait_ge(s_m1, b + 1)
                own.link(dve.tensor_tensor(pos[:, :], m1[:, :], back[:, TJ * b:TJ * b + TJ], ALU.mult))
                own.mark(dve.tensor_tensor(pos[:, :], pos[:, :], tokF[:, TJ * b:TJ * b + TJ], ALU.add))

            def counts(b):
                dve.wait_ge(s_pf, 2 * b + 2)
                own.mark(dve.tensor_tensor_scan(incl[:, :], ones[:, 0:TJ], pR[0][:, TJ:2 * TJ], run[:, 0:1], ALU.mult, ALU.add))

            def ranks(b):
                own.settle()
                own.mark(dve.tensor_copy(run[:, :], incl[:, TJ - 1:TJ]))
                own.link(dve.tensor_tensor(rank[:, :], incl[:, :], pR[0][:, TJ:2 * TJ], ALU.subtract))
                dve.tensor_tensor(rank[:, :], rank[:, :], pR[0][:, 0:TJ], ALU.add).then_inc(s_rk, 1)
                if b == NB - 2:
                    own.link(dve.tensor_scalar(firstf[:, :], run[:, :], -1.0, float((NB - 1) * L), ALU.mult, ALU.add))
                    dve.tensor_copy(firstI[:, :], firstf[:, :]).then_inc(s_first, 1)

            def positions(b):
                dve.wait_ge(s_rk, b + 1)
                wait(dve, s_sc1, 16 * TJ * b)
                dve.tensor_tensor(posI[:, b % 2, :], pos[:, :], rank[:, :], ALU.subtract).then_inc(s_pos, 1)

            def top_weight(b):
                dve.wait_ge(s_ea, b + 1)
                own.link(dve.tensor_scalar(den[:, :], eal[:, :], 1.0, None, ALU.add))
                dve.wait_ge(s_pad, 1)
                dve.reciprocal(res[:, b % 2, :, DM:DM + 1], den[:, :].rearrange("p (j o) -> p j o", o=1)).then_inc(s_tw, 1)

            def clamp(g, sg, ab, signal):
                own.link(dve.tensor_scalar(sg, g, 0.0, 2.0, ALU.is_ge, ALU.mult))
                own.link(dve.scalar_tensor_tensor(ab, g, -1.0, g, ALU.mult, ALU.max))
                own.link(dve.tensor_scalar(ab, ab, 0.25, None, ALU.max))
                dve.scalar_tensor_tensor(g, sg, -1.0, ab, ALU.add, ALU.mult).then_inc(signal, 1)

            def mod_row(r, dst, one):
                dve.wait_ge(s_mm, r + 1)
                return dve.tensor_scalar(dst, pR[r % 2][0:NB, :], one, None, ALU.add)

            def clamp_row(n):
                clamp(modrow[0:NB, n, :], junk[0:NB, :], modrow[0:NB, 0, :], s_mr)

            def columns(lo, hi, n):
                dve.wait_ge(s_mc, n)
                return dve.tensor_copy(cols[:, lo:hi, :, :].rearrange("p n k b -> p (n k b)"),
                                       pX[:, KT * NB * lo:KT * NB * hi])

            own.mark(dve.memset(ones[:, :], 1.0))
            own.mark(dve.memset(run[:, :], 0.0))
            dve.memset(hT[:, :, 0:PAD], 0.0).then_inc(s_dconst, 1)
            dve.wait_ge(s_sil, 1)
            own.link(dve.tensor_scalar(sct[:, :], sc[:, :], 1.0, None, ALU.add))
            own.link(dve.reciprocal(sct[:, :], sct[:, :]))
            dve.tensor_tensor(sc[:, :], c_sb[:, :], sct[:, :], ALU.mult).then_inc(s_silu, 1)
            dve.memset(packed[:, 3 * DM:MODW], 0.0).then_inc(s_dconst, 1)
            dve.memset(eps_col[:, :], EPS).then_inc(s_dconst, 1)
            stats1(0)
            newton1(0)
            mod_row(0, modrow[0:NB, 1, :], 1.0).then_inc(s_mr, 1)
            mod_row(1, modrow[0:NB, 0, :], 0.0).then_inc(s_mr, 1)
            dve.wait_ge(s_wt, 48)
            for k in range(KT):
                ins = dve.tensor_scalar(wdb[:, k, :], ones[:, :], wx_sb[:, k, 2 * S:2 * S + 1], None, ALU.mult)
                if k < KT - 1:
                    own.mark(ins)
                else:
                    ins.then_inc(s_wdb, 1)
            columns(0, 2, 1).then_inc(s_cols, 1)
            own.link(mod_row(2, modrow[0:NB, 2, :], 0.0))
            clamp_row(2)
            dve.wait_ge(s_A, 1)
            dve.tensor_scalar(Acol[:, :], Acol[:, :], -1.0, None, ALU.mult).then_inc(s_An, 1)
            taps = {}
            conv(0, 0, range(KT), taps)
            softplus_residue(0)
            conv(0, 1, range(KT), taps)
            softplus(0)
            conv(0, 2, range(KT), taps)
            columns(2, 3, 2).then_inc(s_cols, 1)
            dve.wait_ge(s_cols, 2)
            for k in range(KT):
                dve.tensor_scalar(Dga[:, k, :], cols[:, 2, k, :], Dv[:, k:k + 1], None, ALU.mult).then_inc(s_Dga, 1)
            for step in newton1_steps(1):
                step()
            dve.wait_ge(s_wr, 16)
            own.link(dve.tensor_tensor(wdiff[:, :], wr[:, 1, :], wr[:, 0, :], ALU.subtract))
            dve.wait_ge(s_dconst, 3)

            for b in range(NB):
                nxt = b + 1 < NB
                scan(b)
                if b == 0:
                    own.link(mod_row(3, packed[0:NB, 0:DM], 1.0))
                    dve.tensor_tensor(packed[0:NB, 2 * DM:3 * DM], packed[0:NB, 0:DM], wdiff[0:NB, :], ALU.mult).then_inc(s_mr, 1)
                wait(dve, s_sc2[b % 2], 16 * TJ * (b // 2))
                taps = {}
                newton_steps = newton1_steps(b + 2) if b + 2 < NB else None
                between = [lambda: conv(b + 1, 0, (0, 1), taps), lambda: conv(b + 1, 0, (2, 3), taps),
                           lambda: conv(b + 1, 1, (0, 1), taps), lambda: conv(b + 1, 1, (2, 3), taps)]
                for j in range(TJ):
                    if nxt:
                        between[j]()
                    residual(b, j)
                    if b + 2 < NB and j == 3:
                        newton_steps[0]()
                    if b == NB - 1 and j < TJ - 1:
                        dve.wait_ge(s_x2, TJ * b + j + 1)
                        own.mark(dve.bn_stats(st2[:, j, :], res[:, b % 2, j, 0:DM]))
                if nxt:
                    for k in range(KT):
                        if k == 2:
                            softplus_residue(b + 1)
                        conv(b + 1, 2, (k,), taps)
                        if newton_steps and k < 3:
                            newton_steps[k + 1]()
                    softplus(b + 1)
                if b == 0:
                    own.link(mod_row(4, packed[0:NB, DM:2 * DM], 0.0))
                    dve.tensor_tensor_reduce(junk[0:NB, :], packed[0:NB, DM:2 * DM], wdiff[0:NB, :], 1.0, 0.0, ALU.mult,
                                             ALU.add, packed[0:NB, 3 * DM:3 * DM + 1]).then_inc(s_mr, 1)
                    dve.wait_ge(s_mr, 5)
                stats2(b)
                newton2(b)
                if b == 0:
                    mod_row(5, modrow[0:NB, 3, :], 0.0).then_inc(s_g5, 1)
                    own.link(dve.tensor_copy(tokF[:, :], tokbat[:, :, 0]))
                    own.link(dve.tensor_scalar(back[:, :], tokF[:, :], -1.0, float(ROWS - 1), ALU.mult, ALU.add))
                if b == NB - 1:
                    dve.wait_ge(s_rs2, b + 1)
                    dve.wait_ge(s_sc1, 16 * TJ * b)
                    for j in DVE_H2:
                        z2_done[j] = own.mark(dve.tensor_scalar(h2[:, j, :], res[:, b % 2, j, 0:DM], rs2[:, j:j + 1],
                                                                nm2[:, j:j + 1], ALU.mult, ALU.add))
                margins(b)
                if b == NB - 1:
                    row_candidates(b)
                    counts(b)
                    ranks(b)
                    positions(b)
                    own.link(dve.tensor_scalar(n0f[:, :], run[:, :], -1.0, float(TOK), ALU.mult, ALU.add))
                    dve.tensor_copy(n0I[:, :], n0f[:, :]).then_inc(s_n0, 1)
                    own.link(dve.tensor_scalar(gapf[:, :], tokF[:, 0:SUB], n0f[:, 0:1], None, ALU.add))
                    dve.tensor_copy(gapI[:, :], gapf[:, :]).then_inc(s_n0, 1)
                    for j in DVE_H2:
                        dve.wait_ge(s_lg, TJ * b + j + 1)
                        own.link(dve.tensor_tensor(h2[:, j, :], h2[:, j, :], bc[:, b, 0:DM], ALU.mult))
                        dve.tensor_tensor(h2[:, j, :], h2[:, j, :], bc[:, b, DM:2 * DM], ALU.add).then_inc(s_h2d, 1)
                    top_weight(b)
                if b == 0:
                    dve.wait_ge(s_g5, 1)
                    clamp_row(3)

            def low_rows(t):
                for s in range(SUB * t, SUB * t + SUB):
                    dve.wait_ge(s_xhi, s + 1)
                    dve.tensor_tensor(XSlo[:, :, P * s:P * s + P], xP[s % 2][:, :].rearrange("p (k t) -> p k t", k=KT),
                                      XShi[:, :, P * s:P * s + P].bitcast(F32), ALU.subtract).then_inc(s_xlo, 1)

            def twice(hb, t):
                i = NT * hb + t
                for m in range(HM):
                    dve.wait_ge(s_relu[m], i + 1)
                    wait(dve, s_af[m], i)
                    dve.tensor_tensor(twice_h[:, m, :], relu_h[:, m, :], hP[m][:, 0:TILE], ALU.add).then_inc(s_q[m], 1)

            def low(hb, t):
                i = NT * hb + t
                for m in range(HM):
                    dve.wait_ge(s_af[m], i + 1)
                    wait(dve, s_au[m], i)
                    dve.tensor_tensor(alo[:, m, :], a_full[:, m, :], ahi[:, m, :].bitcast(F32),
                                      ALU.subtract).then_inc(s_al2[m], 1)

            def accumulate(mode, hb, t):
                i = NT * hb + t
                for s in range(SUB):
                    dve.wait_ge(s_yy[s], i + 1)
                    sub = acc[:, bass.ds(SUB * t + s, 1), :].rearrange("p o d -> p (o d)")
                    if mode == "first":
                        dve.tensor_copy(sub, yP[s][:, :]).then_inc(s_yu[s], 1)
                    else:
                        dve.tensor_tensor(sub, sub, yP[s][:, :], ALU.add).then_inc(s_yu[s], 1)

            def finish_rows(t):
                for s in range(SUB):
                    sub, row = acc[:, SUB * t + s, :], res_row[t % RING][s]
                    dve.wait_ge(s_yu[s], NT * (NHB - 1) + t + 1)
                    dve.wait_ge(s_rr[t % RING][s], 16 * (t // RING + 1))
                    dve.wait_ge(s_gr[t % RING][s], 16 * (t // RING + 1))
                    dve.scalar_tensor_tensor(sub, sub, row[:, DM:DM + 1], gb_row[t % RING][s][:, :], ALU.mult,
                                             ALU.mult).then_inc(s_fin, 1)
                for s in range(SUB):
                    sub, row = acc[:, SUB * t + s, :], res_row[t % RING][s]
                    dve.wait_ge(s_fin, SUB * t + s + 1)
                    dve.tensor_tensor(sub, sub, row[:, 0:DM], ALU.add).then_inc(s_or[s], 1)

            def finish_block(mode, hb):
                twice(hb, 0)
                accumulate(mode, hb - 1, NT - 1)
                low(hb, 0)

            for t in range(FIRST):
                low_rows(t)
            for t in range(NT):
                for n in next_rows(t):
                    low_rows(n)
                if t == FIRST:
                    accumulate("first", 0, t - 1)
                twice(0, t)
                if t == FIRST - 1:
                    low_rows(FIRST)
                if t > 0 and t != FIRST:
                    accumulate("first", 0, t - 1)
                low(0, t)
            finish_block("first", 1)
            with dve.Fori(1, NHB - 1) as hb:
                with dve.Fori(1, NT) as t:
                    twice(hb, t)
                    accumulate("add", hb, t - 1)
                    low(hb, t)
                finish_block("add", hb + 1)
            for t in range(1, NT):
                twice(NHB - 1, t)
                accumulate("add", NHB - 1, t - 1)
                low(NHB - 1, t)
                finish_rows(t - 1)
            accumulate("add", NHB - 1, NT - 1)
            finish_rows(NT - 1)



def kernel(**inputs):
    import concourse.bacc as bacc
    from concourse.bass_utils import run_bass_kernel_spmd as run_spmd

    a = {k.removeprefix("L0_"): np.asarray(v) for k, v in inputs.items()}

    def rows(m):
        return m.reshape(m.shape[0] // P, P, -1).transpose(1, 0, 2)

    fc = a["ffn_w_fc"].reshape(NE, NHB, HB, KT, P).transpose(1, 4, 0, 3, 2).reshape(NHB, P, CH // 2, 512)
    proj = a["ffn_w_proj"].reshape(NE, DM, NHB, HM, P).transpose(2, 4, 0, 3, 1).reshape(NHB, P, CH // 2, 512)
    arrays = {
        "x": a["attn_x"].reshape(NB, TJ, P, DM).transpose(0, 2, 1, 3),
        "cT": rows(a["c"].T).reshape(P, KT * NB),
        "wmod": a["wmod"].reshape(KT, P, 6, DM).transpose(2, 1, 0, 3),
        "wx": rows(a["attn_Wxproj"].T),
        "win": rows(a["attn_Winproj"].T),
        "wout": a["attn_Woutproj"].T,
        "conv_w": rows(a["attn_conv_w"].reshape(DM, TAPS)),
        "conv_b": a["attn_conv_b"].reshape(KT, P).T,
        "A_log": a["attn_A_log"].reshape(S, 1),
        "Dvec": a["attn_D"].reshape(KT, P).T,
        "w_router": a["ffn_w_router"],
        "wffn": np.concatenate([fc, proj], axis=2),
    }
    arrays = {k: np.ascontiguousarray(v) for k, v in arrays.items()}
    nc = bacc.Bacc("TRN2", target_bir_lowering=False, num_devices=1)
    args = [nc.dram_tensor(k, v.shape, mybir.dt.from_np(v.dtype), kind="ExternalInput").ap() for k, v in arrays.items()]
    out = nc.dram_tensor("out", (TOK, DM), F32, kind="ExternalOutput").ap()
    build(nc, *args, out)
    r = run_spmd(nc, [arrays], core_ids=[0])
    return r.results[0]["out"].reshape(NB, L, DM)
```
